# Optimizing a Trainium2 kernel written in Bass

```python
import numpy as np
import jax
import jax.numpy as jnp

def _softmax(x, axis=-1):
    return jax.nn.softmax(x, axis=axis)

def _gelu(x):
    return jax.nn.gelu(x, approximate=True)

def _silu(x):
    return jax.nn.silu(x)

def _sigmoid(x):
    return jax.nn.sigmoid(x)

def _layernorm(x, axis=-1, eps=1e-05):
    m = jnp.mean(x, axis=axis, keepdims=True)
    v = jnp.var(x, axis=axis, keepdims=True)
    return (x - m) / jnp.sqrt(v + eps)

def _scatter_add(tgt, idx, src, axis=0):
    return tgt.at[idx].add(src)

def _segment_sum(src, seg, n):
    return jax.ops.segment_sum(src, seg, n)
kernel_name = 'mk_xattn_ffn_d2_seqx_r4_7c2863'

def setup_inputs(seed: int=0):
    np.random.seed(seed)
    _w = jnp.asarray

    def _rec_inputs():
        import jax
        import jax.numpy as jnp
        _rk = jax.random.key(seed)
        x = -0.0003929 + 0.9999 * jax.random.normal(jax.random.fold_in(_rk, 1), (8, 256, 256), jnp.float32)
        _lenS = 256 - jax.random.randint(jax.random.fold_in(_rk, 7), (8,), 0, max(1, 256 // 4) + 1, jnp.int32)
        _lenS2 = 256 - jax.random.randint(jax.random.fold_in(_rk, 8), (8,), 0, max(1, 256 // 4) + 1, jnp.int32)
        _ctx_768P = jax.random.normal(jax.random.fold_in(_rk, 11), (8, 16, 192), jnp.float32)
        _ctx_768c = jax.random.dirichlet(jax.random.fold_in(_rk, 511), 0.3 * jnp.ones((16,), jnp.float32), (8, 256))
        _ctx_768t = jnp.einsum('bsk,bkd->bsd', _ctx_768c, _ctx_768P)
        _ctx_768t = _ctx_768t * jax.lax.rsqrt(jnp.mean(jnp.square(_ctx_768t)) + 1e-12) * 0.953939
        ctx_768 = 0.00095986 + 0.999812 * (_ctx_768t + 0.3 * jax.random.normal(jax.random.fold_in(_rk, 611), (8, 256, 192), jnp.float32))
        _validS = jnp.arange(256)[None, :] < _lenS[:, None]
        _validS2 = jnp.arange(256)[None, :] < _lenS2[:, None]
        _causal = jnp.tril(jnp.ones((256, 256), dtype=bool))
        mask_BxS2_bf1 = jnp.ones((8, 256), dtype=bool)
        return (x, ctx_768, mask_BxS2_bf1)
    x, ctx_768, mask_BxS2_bf1 = _rec_inputs()

    def _L0_xattn_setup():
        import jax, jax.numpy as jnp
        import numpy as np
        DIM = 256
        CTX_DIM = 192
        HEADS = 16
        key = jax.random.key(seed)
        ks = jax.random.split(key, 7)
        B, N, M = (4, 1024, 64)
        x = jax.random.normal(ks[0], (B, N, DIM), dtype=jnp.float32)
        context = jax.random.normal(ks[1], (B, M, CTX_DIM), dtype=jnp.float32)
        context_mask = jnp.ones((B, M), dtype=bool)
        s_d = 1.0 / np.sqrt(DIM)
        s_c = 1.0 / np.sqrt(CTX_DIM)
        Wq = jax.random.normal(ks[2], (DIM, DIM), dtype=jnp.float32) * s_d
        Wk = jax.random.normal(ks[3], (CTX_DIM, DIM), dtype=jnp.float32) * s_c
        Wv = jax.random.normal(ks[4], (CTX_DIM, DIM), dtype=jnp.float32) * s_c
        Wo = jax.random.normal(ks[5], (DIM, DIM), dtype=jnp.float32) * s_d
        return {'x': x, 'context': context, 'context_mask': context_mask, 'Wq': Wq, 'Wk': Wk, 'Wv': Wv, 'Wo': Wo}
    _L0_xattn_all = _L0_xattn_setup()
    _L0_xattn_in = {k: v for k, v in _L0_xattn_all.items() if k in ('Wq', 'Wk', 'Wv', 'Wo')}
    del _L0_xattn_all

    def _L0_ffn_setup():
        import jax, jax.numpy as jnp
        import numpy as np
        B, SEQ, DIM = (2, 1024, 256)
        E, S = (8, 128)
        HID = 4 * DIM
        SCALE = DIM ** 0.5

        def rmsnorm(x, gamma):
            n = jnp.linalg.norm(x, axis=-1, keepdims=True)
            return x / jnp.maximum(n, 1e-12) * SCALE * gamma
        key = jax.random.key(seed)
        ks = jax.random.split(key, 4)
        w_init = lambda k, shape: jax.random.normal(k, shape, dtype=jnp.float32) * 0.02
        return {'x': jax.random.normal(ks[0], (B, SEQ, DIM), dtype=jnp.float32), 'norm_gamma': jnp.ones((DIM,), jnp.float32), 'slot_norm_gamma': jnp.ones((DIM,), jnp.float32), 'slot_embeds': jax.random.normal(ks[1], (E, S, DIM), dtype=jnp.float32), 'w1': w_init(ks[2], (E, DIM, HID)), 'b1': jnp.zeros((E, HID), jnp.float32), 'w2': w_init(ks[3], (E, HID, DIM)), 'b2': jnp.zeros((E, DIM), jnp.float32)}
    _L0_ffn_all = _L0_ffn_setup()
    _L0_ffn_in = {k: v for k, v in _L0_ffn_all.items() if k in ('norm_gamma', 'slot_norm_gamma', 'slot_embeds', 'w1', 'b1', 'w2', 'b2')}
    del _L0_ffn_all

    def _L1_xattn_setup():
        import jax, jax.numpy as jnp
        import numpy as np
        N_HEADS = 16
        D_HEAD = 64
        key = jax.random.key(seed)
        ks = jax.random.split(key, 7)
        B, SQ, SKV = (2, 512, 512)
        D_MODEL, D_COND, D_ATTN = (256, 192, N_HEADS * D_HEAD)
        return {'x': jax.random.normal(ks[0], (B, SQ, D_MODEL), jnp.float32), 'cond': jax.random.normal(ks[1], (B, SKV, D_COND), jnp.float32), 'w_q': jax.random.normal(ks[2], (D_MODEL, D_ATTN), jnp.float32) * D_MODEL ** (-0.5), 'w_k': jax.random.normal(ks[3], (D_COND, D_ATTN), jnp.float32) * D_COND ** (-0.5), 'w_v': jax.random.normal(ks[4], (D_COND, D_ATTN), jnp.float32) * D_COND ** (-0.5), 'w_out': jax.random.normal(ks[5], (D_ATTN, D_MODEL), jnp.float32) * D_ATTN ** (-0.5), 'b_out': jnp.zeros((D_MODEL,), jnp.float32)}
    _L1_xattn_all = _L1_xattn_setup()
    _L1_xattn_in = {k: v for k, v in _L1_xattn_all.items() if k in ('w_q', 'w_k', 'w_v', 'w_out', 'b_out')}
    del _L1_xattn_all

    def _L1_ffn_setup():
        import jax, jax.numpy as jnp
        import numpy as np
        DIM = 256

        def _reference_tuple_inner(x, W_r, W_k, W_v, mu_r, mu_k):
            B, T, C = x.shape
            x_prev = jnp.concatenate([jnp.zeros((B, 1, C), x.dtype), x[:, :-1, :]], axis=1)
            xr = mu_r * x + (1.0 - mu_r) * x_prev
            xk = mu_k * x + (1.0 - mu_k) * x_prev
            r = jax.nn.sigmoid(jnp.einsum('btc,dc->btd', xr, W_r))
            k = jnp.einsum('btc,dc->btd', xk, W_k)
            k_act = jnp.square(jax.nn.relu(k))
            out = r * jnp.einsum('btc,dc->btd', k_act, W_v)
            new_state = x[:, -1, :]
            return (out, new_state)
        key = jax.random.key(seed)
        ks = jax.random.split(key, 6)
        B, T, C = (8, 512, DIM)
        x = jax.random.normal(ks[0], (B, T, C), dtype=jnp.float32)
        s = 1.0 / np.sqrt(C)
        W_r = jax.random.uniform(ks[1], (C, C), jnp.float32, -s, s)
        W_k = jax.random.uniform(ks[2], (C, C), jnp.float32, -s, s)
        W_v = jax.random.uniform(ks[3], (C, C), jnp.float32, -s, s)
        mu_r = jax.random.uniform(ks[4], (C,), jnp.float32)
        mu_k = jax.random.uniform(ks[5], (C,), jnp.float32)
        return {'x': x, 'W_r': W_r, 'W_k': W_k, 'W_v': W_v, 'mu_r': mu_r, 'mu_k': mu_k}
    _L1_ffn_all = _L1_ffn_setup()
    _L1_ffn_in = {k: v for k, v in _L1_ffn_all.items() if k in ('W_r', 'W_k', 'W_v', 'mu_r', 'mu_k')}
    del _L1_ffn_all
    return {'x': x, 'ctx_768': ctx_768, 'mask_BxS2_bf1': mask_BxS2_bf1, 'L0_xattn_Wq': _L0_xattn_in['Wq'], 'L0_xattn_Wk': _L0_xattn_in['Wk'], 'L0_xattn_Wv': _L0_xattn_in['Wv'], 'L0_xattn_Wo': _L0_xattn_in['Wo'], 'L0_ffn_norm_gamma': _L0_ffn_in['norm_gamma'], 'L0_ffn_slot_norm_gamma': _L0_ffn_in['slot_norm_gamma'], 'L0_ffn_slot_embeds': _L0_ffn_in['slot_embeds'], 'L0_ffn_w1': _L0_ffn_in['w1'], 'L0_ffn_b1': _L0_ffn_in['b1'], 'L0_ffn_w2': _L0_ffn_in['w2'], 'L0_ffn_b2': _L0_ffn_in['b2'], 'L1_xattn_w_q': _L1_xattn_in['w_q'], 'L1_xattn_w_k': _L1_xattn_in['w_k'], 'L1_xattn_w_v': _L1_xattn_in['w_v'], 'L1_xattn_w_out': _L1_xattn_in['w_out'], 'L1_xattn_b_out': _L1_xattn_in['b_out'], 'L1_ffn_W_r': _L1_ffn_in['W_r'], 'L1_ffn_W_k': _L1_ffn_in['W_k'], 'L1_ffn_W_v': _L1_ffn_in['W_v'], 'L1_ffn_mu_r': _L1_ffn_in['mu_r'], 'L1_ffn_mu_k': _L1_ffn_in['mu_k']}

def reference(x, ctx_768, mask_BxS2_bf1, L0_xattn_Wq, L0_xattn_Wk, L0_xattn_Wv, L0_xattn_Wo, L0_ffn_norm_gamma, L0_ffn_slot_norm_gamma, L0_ffn_slot_embeds, L0_ffn_w1, L0_ffn_b1, L0_ffn_w2, L0_ffn_b2, L1_xattn_w_q, L1_xattn_w_k, L1_xattn_w_v, L1_xattn_w_out, L1_xattn_b_out, L1_ffn_W_r, L1_ffn_W_k, L1_ffn_W_v, L1_ffn_mu_r, L1_ffn_mu_k):
    import jax
    import jax.numpy as jnp

    def _L0_xattn_ref(x, context, context_mask, Wq, Wk, Wv, Wo):
        import jax, jax.numpy as jnp
        import numpy as np
        DIM = 256
        CTX_DIM = 192
        HEADS = 16
        B, N, _ = x.shape
        M = context.shape[1]
        hd = DIM // HEADS
        scale = hd ** (-0.5)
        q = (x @ Wq).reshape(B, N, HEADS, hd).transpose(0, 2, 1, 3)
        k = (context @ Wk).reshape(B, M, HEADS, hd).transpose(0, 2, 1, 3)
        v = (context @ Wv).reshape(B, M, HEADS, hd).transpose(0, 2, 1, 3)
        scores = jnp.einsum('bhid,bhjd->bhij', q, k) * scale
        max_neg = -jnp.finfo(scores.dtype).max
        scores = jnp.where(context_mask[:, None, None, :], scores, max_neg)
        attn = jax.nn.softmax(scores, axis=-1)
        out = jnp.einsum('bhij,bhjd->bhid', attn, v)
        out = out.transpose(0, 2, 1, 3).reshape(B, N, DIM)
        return out @ Wo

    def _L0_ffn_ref(x, norm_gamma, slot_norm_gamma, slot_embeds, w1, b1, w2, b2):
        import jax, jax.numpy as jnp
        import numpy as np
        B, SEQ, DIM = (2, 1024, 256)
        E, S = (8, 128)
        HID = 4 * DIM
        SCALE = DIM ** 0.5

        def rmsnorm(x, gamma):
            n = jnp.linalg.norm(x, axis=-1, keepdims=True)
            return x / jnp.maximum(n, 1e-12) * SCALE * gamma
        xn = rmsnorm(x, norm_gamma)
        sn = rmsnorm(slot_embeds, slot_norm_gamma)
        logits = jnp.einsum('bnd,esd->bnes', xn, sn)
        dispatch = jax.nn.softmax(logits, axis=1)
        b, n, e, s = logits.shape
        combine = jax.nn.softmax(logits.reshape(b, n, e * s), axis=-1)
        slots = jnp.einsum('bnd,bnes->besd', xn, dispatch)
        h = jnp.einsum('besd,edh->besh', slots, w1) + b1[None, :, None, :]
        h = jax.nn.gelu(h, approximate=False)
        eo = jnp.einsum('besh,ehd->besd', h, w2) + b2[None, :, None, :]
        eo = eo.reshape(b, e * s, DIM)
        out = jnp.einsum('bmd,bnm->bnd', eo, combine)
        return out

    def _L1_xattn_ref(x, cond, w_q, w_k, w_v, w_out, b_out):
        import jax, jax.numpy as jnp
        import numpy as np
        N_HEADS = 16
        D_HEAD = 64
        B, SQ, _ = x.shape
        SKV = cond.shape[1]
        scale = D_HEAD ** (-0.5)
        q = (x @ w_q).reshape(B, SQ, N_HEADS, D_HEAD)
        k = (cond @ w_k).reshape(B, SKV, N_HEADS, D_HEAD)
        v = (cond @ w_v).reshape(B, SKV, N_HEADS, D_HEAD)
        attn = jnp.einsum('bqhd,bkhd->bhqk', q, k) * scale
        attn = jax.nn.softmax(attn, axis=-1)
        out = jnp.einsum('bhqk,bkhd->bqhd', attn, v).reshape(B, SQ, N_HEADS * D_HEAD)
        return out @ w_out + b_out

    def _L1_ffn_ref(x, W_r, W_k, W_v, mu_r, mu_k):
        import jax, jax.numpy as jnp
        import numpy as np
        DIM = 256

        def _reference_tuple_inner(x, W_r, W_k, W_v, mu_r, mu_k):
            B, T, C = x.shape
            x_prev = jnp.concatenate([jnp.zeros((B, 1, C), x.dtype), x[:, :-1, :]], axis=1)
            xr = mu_r * x + (1.0 - mu_r) * x_prev
            xk = mu_k * x + (1.0 - mu_k) * x_prev
            r = jax.nn.sigmoid(jnp.einsum('btc,dc->btd', xr, W_r))
            k = jnp.einsum('btc,dc->btd', xk, W_k)
            k_act = jnp.square(jax.nn.relu(k))
            out = r * jnp.einsum('btc,dc->btd', k_act, W_v)
            new_state = x[:, -1, :]
            return (out, new_state)
        return _reference_tuple_inner(x, W_r, W_k, W_v, mu_r, mu_k)[0]
    x = x + _L0_xattn_ref(_layernorm(x, axis=-1), ctx_768, mask_BxS2_bf1, L0_xattn_Wq, L0_xattn_Wk, L0_xattn_Wv, L0_xattn_Wo)
    x = x + _L0_ffn_ref(_layernorm(x, axis=-1), L0_ffn_norm_gamma, L0_ffn_slot_norm_gamma, L0_ffn_slot_embeds, L0_ffn_w1, L0_ffn_b1, L0_ffn_w2, L0_ffn_b2)
    x = x + _L1_xattn_ref(_layernorm(x, axis=-1), ctx_768, L1_xattn_w_q, L1_xattn_w_k, L1_xattn_w_v, L1_xattn_w_out, L1_xattn_b_out)
    x = x + _L1_ffn_ref(_layernorm(x, axis=-1), L1_ffn_W_r, L1_ffn_W_k, L1_ffn_W_v, L1_ffn_mu_r, L1_ffn_mu_k)
    return x

_drawn_inputs = setup_inputs


def setup_inputs(seed=0):
    import zlib

    import numpy as np

    out = dict(_drawn_inputs(seed))
    spreads = {'L0_ffn_norm_gamma': (1.0, 0.2),
     'L0_ffn_slot_norm_gamma': (1.0, 0.2),
     'L0_ffn_b1': (0.0, 0.277),
     'L0_ffn_b2': (0.0, 0.1),
     'L1_xattn_b_out': (0.0, 0.1)}
    factors = {'L1_ffn_W_r': 3.291, 'L1_ffn_mu_r': 8.0}
    for name, (base, spread) in spreads.items():
        noise = np.random.default_rng([zlib.crc32(name.encode()), seed]).standard_normal(out[name].shape)
        drawn = base * np.exp(spread * noise) if base else spread * noise
        out[name] = jnp.asarray(drawn.astype(out[name].dtype))
    for name, factor in factors.items():
        out[name] = (out[name] * factor).astype(out[name].dtype)
    return out
```

```python
from contextlib import ExitStack

import concourse.bass as bass
from concourse import mybir

F32 = mybir.dt.float32
F32R = mybir.dt.float32r
U8 = mybir.dt.uint8
I32 = mybir.dt.int32
ALU = mybir.AluOpType
ACT = mybir.ActivationFunctionType
AX = mybir.AxisListType

P = 128
MASKED = 2.0 ** 100
LN_EPS = 1e-5
EXP_MAX = 80.0
RMS_FLOOR = 1e-24
ROOT_GUESS = float(0x5F375A00)
LN_STEPS = 14
RMS_STEPS = 15



def terms(a_hi, a_lo, b_hi, b_lo):
    return ((a_hi, b_hi), (a_lo, b_hi), (a_hi, b_lo))


def halves(bank):
    return bank.rearrange("p (a n) -> p a n", a=2)


class Norm:

    def __init__(self, sb, sem, name, n):
        self.n = n
        self.bn = sb(f"{name}_bn", [P, n, 6], F32)
        self.mv = sb(f"{name}_mv", [P, n, 2], F32)
        self.v = sb(f"{name}_v", [P, 2, n], F32)
        self.half = sb(f"{name}_half", [P, n], I32)
        self.root = sb(f"{name}_root", [P, 3, n], F32)
        self.step = sem(f"{name}_step")


class Buffers:

    def __init__(self, sb, sem, i, KC, N, D):
        NT, DT = N // P, D // P
        self.x_in = sb(f"x_in{i}", [P, NT, D], F32)
        self.xn = sb(f"xn{i}", [P, NT, D], F32)
        self.xT_hi = sb(f"xT_hi{i}", [P, DT, N], F32R)
        self.xT_lo = sb(f"xT_lo{i}", [P, DT, N], F32R)
        self.ctxT = sb(f"ctxT{i}", [KC, 2, N], F32)
        self.ctxT_hi = sb(f"ctxT_hi{i}", [KC, 2, N], F32R)
        self.ctxT_lo = sb(f"ctxT_lo{i}", [KC, 2, N], F32R)
        self.ex = sb(f"ex{i}", [P, 4, 2, 256], F32)
        self.prob_hi = sb(f"prob_hi{i}", [P, 2, 2, 256], F32R)
        self.prob_lo = sb(f"prob_lo{i}", [P, 2, 2, 256], F32R)
        self.neg_max = sb(f"neg_max{i}", [P, 4, 2], F32)
        self.row_sum = sb(f"row_sum{i}", [P, 4, 2], F32)
        self.row_inv = sb(f"row_inv{i}", [P, 4, 2], F32)
        self.oT_hi = sb(f"oT_hi{i}", [P, 2, N], F32R)
        self.oT_lo = sb(f"oT_lo{i}", [P, 2, N], F32R)
        self.scores_ready = sem(f"scores_ready{i}")
        self.max_ready = sem(f"max_ready{i}")
        self.exp_ready = sem(f"exp_ready{i}")
        self.inv_ready = sem(f"inv_ready{i}")
        self.norm_ready = sem(f"norm_ready{i}")
        self.trans_ready = sem(f"trans_ready{i}")
        self.prob_hi_ready = sem(f"prob_hi_ready{i}")
        self.prob_lo_ready = sem(f"prob_lo_ready{i}")
        self.pv_done = sem(f"pv_done{i}")
        self.oT_hi_ready = sem(f"oT_hi_ready{i}")
        self.oT_lo_ready = sem(f"oT_lo_ready{i}")
        self.oproj_done = sem(f"oproj_done{i}")
        self.sum_taken = sem(f"sum_taken{i}")
        self.g_ready = sem(f"g_ready{i}")
        self.g_hi = sem(f"g_hi{i}")
        self.g_lo = sem(f"g_lo{i}")
        self.ctx_hi_made = sem(f"ctx_hi_made{i}")
        self.ctx_lo_made = sem(f"ctx_lo_made{i}")
        self.x_loaded = sem(f"x_loaded{i}")
        self.ctx_loaded = sem(f"ctx_loaded{i}")
        self.xn_made = sem(f"xn_made{i}")


def xattn_ffn_kernel(nc, a, out):
    B, N, D = a["x"].shape
    C = a["ctxT"].shape[1]
    KC = C // 2
    H = 16
    HD0 = D // H
    A1 = a["w_q"].shape[1]
    HD1 = A1 // H
    E, S, _ = a["slots"].shape
    HID = a["w1"].shape[2]
    NT = N // P
    DT = D // P
    G = 4
    GH = H // G
    VW = P + 32
    M = E * S
    PAIRS = E // 2
    HT = HID // P
    HP = H // 2
    BH = B // 2
    assert N == 256 and D == 256 and S == P and HD0 == 16 and HD1 == 64 and B == 8 and HT == 8

    x1_dram = nc.dram_tensor("x1_dram", (B, P, NT, D), F32, kind="Internal").ap()
    slots_dram = nc.dram_tensor("slots_dram", (E, P, DT, B, S), F32, kind="Internal").ap()
    comb_dram = nc.dram_tensor("comb_dram", (B, P, E, N), F32, kind="Internal").ap()
    eo_dram = nc.dram_tensor("eo_dram", (E, P, B, D), F32, kind="Internal").ap()

    with ExitStack() as ctx:
        place = ExitStack()

        def sb(name, shape, dt):
            return place.enter_context(nc.sbuf_tensor(name, shape, dt))

        def sem(name):
            return ctx.enter_context(nc.semaphore(name))

        ps_s = ctx.enter_context(nc.psum_tensor("ps_s", [P, 2, 512], F32))
        ps_t = ctx.enter_context(nc.psum_tensor("ps_t", [P, 2, 512], F32))
        ps_o = ctx.enter_context(nc.psum_tensor("ps_o", [P, 2, 512], F32))
        ps_yg = ctx.enter_context(nc.psum_tensor("ps_yg", [P, 2, 512], F32))
        ps_y = ps_yg[:, 0, :]
        ps_g = ps_yg[:, 1, :]

        ident = ctx.enter_context(nc.sbuf_tensor("ident", [P, P], F32))

        u1 = Buffers(sb, sem, "_1", KC, N, D)
        slot_norm = Norm(sb, sem, "slot_norm", E)
        x_norm = Norm(sb, sem, "x_norm", NT)
        r_norm = Norm(sb, sem, "r_norm", NT)
        x_res = sb("x_res", [P, NT, D], F32)
        wq0 = sb("wq0", [P, 2, DT, 2 * D], F32R)
        wk0 = sb("wk0", [KC, 2, 2, 2 * D], F32R)
        wv0 = sb("wv0", [KC, 2, 2, D], F32R)
        wo0 = sb("wo0", [P, 2, G, D], F32R)
        snT = sb("snT", [P, 2, DT, M], F32R)
        raw0 = sb("raw0", [P, 3584], F32)
        slot_raw = sb("slot_raw", [P, E, D], F32)
        rT_hi = sb("rT_hi", [P, DT, N], F32R)
        rT_lo = sb("rT_lo", [P, DT, N], F32R)
        gamma = sb("gamma_sb", [P, D], F32)
        gamma_s = sb("gamma_s_sb", [P, D], F32)
        lo_rows = sb("lo_rows_sb", [P, 1], F32)
        ones = sb("ones", [P, P], F32R)
        mask_u8 = sb("mask_u8", [P, B, N], U8)
        mask_bias = sb("mask_bias", [P, 2, N], F32R)
        q_full = sb("q_full", [P, 2, N], F32R)
        q_mix = sb("q_mix", [P, G, N], F32R)
        k_hi = sb("k_hi", [P, G, N], F32R)
        k_lo = sb("k_lo", [P, G, N], F32R)
        v_pad = sb("v_pad", [P, NT, G, GH * VW], F32R)
        x1 = sb("x1", [P, NT, D], F32)
        xc = sb("xc", [P, NT, D], F32)
        xr = sb("xr", [P, NT, D], F32)
        xr_hi = sb("xr_hi", [P, NT, D], F32R)
        xr_lo = sb("xr_lo", [P, NT, D], F32R)
        logit = sb("logit", [P, NT, M], F32)
        comb = sb("comb", [P, NT, M], F32)
        comb_stat = sb("comb_stat", [P, 3, NT], F32)
        combT = sb("combT", [P, E, N], F32)
        slot_out = sb("slot_out", [P, PAIRS, DT, N], F32)
        place.close()

        w1_raw = sb("w1_raw", [P, DT, HID], F32)
        w2_raw = sb("w2_raw", [P, HT, D], F32)
        sl_raw = sb("sl_raw", [P, DT, B * S], F32)
        w1_s = sb("w1_s", [P, 2, DT, HID], F32R)
        w2_s = sb("w2_s", [P, 2, HT, D], F32R)
        sl_s = sb("sl_s", [P, 2, DT, B * S], F32R)
        b1_sb = sb("b1_sb", [P, HT], F32)
        b2_sb = sb("b2_sb", [P, D], F32)
        h_raw = sb("h_raw", [P, 2, 512], F32)
        h_hi = sb("h_hi", [P, 4, 512], F32R)
        h_lo = sb("h_lo", [P, 4, 512], F32R)
        eo = sb("eo", [P, 2, 2, 2, D], F32)
        place.close()

        u3 = Buffers(sb, sem, "_3", KC, N, D)
        x2_norm = Norm(sb, sem, "x2_norm", NT)
        x3_norm = Norm(sb, sem, "x3_norm", NT)
        wq1 = sb("wq1", [P, 2, DT, A1], F32R)
        wk1 = sb("wk1", [KC, 2, 2, A1], F32R)
        wv1 = sb("wv1", [KC, 2, 2, A1], F32R)
        wo1 = sb("wo1", [P, 2, HP, D], F32R)
        wf = sb("wf_sb", [P, 2, 3, DT, D], F32R)
        comb_raw = sb("comb_raw", [P, E, N], F32)
        eo_raw = sb("eo_raw", [P, E, D], F32)
        qk_hi = sb("qk_hi", [P, 2, 2, N], F32R)
        qk_lo = sb("qk_lo", [P, 2, 2, N], F32R)
        x2_half = sb("x2_half", [P, NT, D], F32)
        x2 = sb("x2", [P, NT, D], F32)
        x2_bias = sb("x2_bias", [P, NT, D], F32)
        x2_res = sb("x2_res", [P, NT, D], F32)
        x3n = sb("x3n", [P, NT, D], F32)
        x3 = sb("x3", [P, NT, D], F32)
        b_out = sb("b_out_sb", [P, D], F32)
        mu = sb("mu_sb", [P, 2, 2, DT], F32)
        xs = sb("xs", [P, DT, N + 1], F32)
        gate = sb("gate", [P, NT, D], F32)
        scratch = sb("scratch", [P, 2, DT, N], F32)
        ka_hi = sb("ka_hi", [P, DT, N], F32R)
        ka_lo = sb("ka_lo", [P, DT, N], F32R)
        y_out = sb("y_out", [P, NT, D], F32)
        comb_s = sb("comb_s", [P, 2, E // 2, N], F32R)
        eo_s = sb("eo_s", [P, 2, E // 2, D], F32R)
        v1_hi = sb("v1_hi", [P, NT, A1], F32R)
        v1_lo = sb("v1_lo", [P, NT, A1], F32R)
        mixed = sb("mixed", [P, 2, DT, N], F32)
        mix_hi = sb("mix_hi", [P, 2, DT, N], F32R)
        mix_lo = sb("mix_lo", [P, 2, DT, N], F32R)
        place.close()

        dve_passed, sp_passed = sem("dve_passed"), sem("sp_passed")
        part_done = [sem(f"part_done{i}") for i in range(2)]
        wq0_loaded, wk0_loaded, wv0_loaded, wo0_loaded = (sem(f"{n}0_loaded") for n in ("wq", "wk", "wv", "wo"))
        slots_loaded = sem("slots_loaded")
        small_loaded = sem("small_loaded")
        consts_made = sem("consts_made")
        w0_hi = sem("w0_hi")
        w0_lo = sem("w0_lo")
        slots_normed = sem("slots_normed")
        snT_ready = sem("snT_ready")
        snT_hi = sem("snT_hi")
        snT_lo = sem("snT_lo")
        res_loaded = sem("res_loaded")
        mask_made = sem("mask_made")
        x1_stored = sem("x1_stored")
        xc_made = sem("xc_made")
        xr_made = sem("xr_made")
        xr_hi_made = sem("xr_hi_made")
        xr_lo_made = sem("xr_lo_made")
        cmax_ready = sem("cmax_ready")
        cexp_ready = sem("cexp_ready")
        cinv_ready = sem("cinv_ready")
        comb_ready = sem("comb_ready")
        comb_stored = sem("comb_stored")
        slot_copied = sem("slot_copied")
        slots_stored = sem("slots_stored")
        sl_loaded = sem("sl_loaded")
        w1_loaded = sem("w1_loaded")
        w2_loaded = sem("w2_loaded")
        b_loaded = sem("b_loaded")
        e_hi = sem("e_hi")
        e_lo_dve = sem("e_lo_dve")
        e_lo_pool = sem("e_lo_pool")
        h_ready = sem("h_ready")
        gelu_done = sem("gelu_done")
        h_hi_made = sem("h_hi_made")
        h_lo_made = sem("h_lo_made")
        eo_part = sem("eo_part")
        eo_made = sem("eo_made")
        eo_stored = sem("eo_stored")
        raw_loaded = [sem("raw_loaded0"), sem("raw_loaded1")]
        w3_hi = sem("w3_hi")
        w3_lo = sem("w3_lo")
        tables_loaded = sem("tables_loaded")
        tables_made = sem("tables_made")
        comb_loaded = sem("comb_loaded")
        eo_loaded = sem("eo_loaded")
        cs_hi = sem("cs_hi")
        cs_lo = sem("cs_lo")
        es_lo = sem("es_lo")
        x2_made = sem("x2_made")
        x2_moved = sem("x2_moved")
        x3n_made = sem("x3n_made")
        mix_part_made = sem("mix_part_made")
        x2_biased = sem("x2_biased")
        mix_made = sem("mix_made")
        mix_hi_made = sem("mix_hi_made")
        mix_lo_made = sem("mix_lo_made")
        gate_exp = sem("gate_exp")
        gate_step = sem("gate_step")
        ksq_done = sem("ksq_done")
        ka_hi_made = sem("ka_hi_made")
        ka_lo_made = sem("ka_lo_made")
        out_made = sem("out_made")
        out_stored = sem("out_stored")

        block = ctx.enter_context(nc.Block())

        NU1 = H + PAIRS
        SPLIT_STEPS = (0, 1, 3, 4)
        HU = 2 * HT
        NSPLIT = 10

        def at(b, per, k):
            return b * per + max(k, 0)

        def end_part(engine, i):
            engine.drain().then_inc(part_done[i], 1)
            engine.wait_ge(part_done[i], 5)

        def pe_transposes(src, bank):
            for c in range(DT):
                for t in range(NT):
                    last = nc.tensor.transpose(halves(bank)[:, c, t * P:t * P + P], src[:, t, c * P:c * P + P],
                                               ident[:, :])
            return last

        def since(v):
            return max(v, 0) if isinstance(v, int) else v

        def pe_unit_transposes(pe, w, u, m):
            pe.wait_ge(w.norm_ready, since(u + 1))
            pe.wait_ge(w.prob_lo_ready, since(u - 1))
            bank = halves(ps_t[:, m % 2, :])
            for k in range(2):
                for q in range(2):
                    last = nc.tensor.transpose(bank[:, k, q * P:q * P + P], w.ex[:, m, q, k * P:k * P + P],
                                               ident[:, :])
            last.then_inc(w.trans_ready, 1)

        def pe_out_proj(pe, w, b, g, groups, wo):
            pe.wait_ge(w.oT_hi_ready, b * groups + g + 1)
            pe.wait_ge(w.oT_lo_ready, b * groups + g + 1)
            if g == 0:
                pe.wait_ge(w.sum_taken, b)
            for t in range(NT):
                tt = slice(t * P, t * P + P)
                for i, (l, r) in enumerate(terms(w.oT_hi[:, g % 2, tt], w.oT_lo[:, g % 2, tt],
                                                 wo[:, 0, g, :], wo[:, 1, g, :])):
                    last = nc.tensor.matmul(halves(ps_y)[:, t, :], l, r, start=g == 0 and t == 0 and i == 0,
                                            stop=g == groups - 1 and i == 2, skip_group_check=True)
            last.then_inc(w.oproj_done, 1)

        def act_unit_exp(act, w, u, m):
            act.wait_ge(w.max_ready, since(u + 1))
            act.wait_ge(w.trans_ready, since(u - 3))
            act.wait_ge(w.inv_ready, since(u - 3))
            for q in range(2):
                last = nc.scalar.activation(w.ex[:, m, q, :], halves(ps_s[:, m % 2, :])[:, q, :], ACT.Exp,
                                            bias=w.neg_max[:, m, q:q + 1], accum_out=w.row_sum[:, m, q:q + 1])
            last.then_inc(w.exp_ready, 1)

        def act_unit_hi(act, w, u, m):
            act.wait_ge(w.trans_ready, since(u + 1))
            act.wait_ge(w.pv_done, since(u - 1))
            nc.scalar.activation(w.prob_hi[:, m % 2, :, :], halves(ps_t[:, m % 2, :]),
                                 ACT.Copy).then_inc(w.prob_hi_ready, 1)

        def dve_unit_max(dve, w, u, m):
            dve.wait_ge(w.scores_ready, since(u + 1))
            dve.wait_ge(w.exp_ready, since(u - 3))
            nc.vector.tensor_reduce(w.neg_max[:, m, :], halves(ps_s[:, m % 2, :]), AX.X, ALU.max,
                                    negate=True).then_inc(w.max_ready, 1)

        def dve_unit_inv(dve, w, u, m):
            dve.wait_ge(w.exp_ready, since(u + 1))
            dve.wait_ge(w.norm_ready, since(u - 3))
            nc.vector.reciprocal(w.row_inv[:, m, :], w.row_sum[:, m, :]).then_inc(w.inv_ready, 1)

        def dve_lo(dst, full, hi):
            return nc.vector.tensor_tensor(dst, full, hi.bitcast(F32), ALU.subtract)

        def dve_unit_lo(dve, w, u, m):
            dve.wait_ge(w.prob_hi_ready, since(u + 1))
            dve.wait_ge(w.pv_done, since(u - 1))
            dve_lo(w.prob_lo[:, m % 2, :, :], halves(ps_t[:, m % 2, :]),
                   w.prob_hi[:, m % 2, :, :]).then_inc(w.prob_lo_ready, 1)

        def pool_unit_norm(pool, w, u, m):
            pool.wait_ge(w.inv_ready, since(u + 1))
            nc.gpsimd.tensor_tensor(w.ex[:, m, :, :], w.ex[:, m, :, :],
                                    w.row_inv[:, m, :].unsqueeze(2).to_broadcast([P, 2, 256]),
                                    ALU.mult).then_inc(w.norm_ready, 1)

        def dve_stats(dve, r, x, c):
            for t in range(r.n):
                last = nc.vector.bn_stats(r.bn[:, t, :], x[:, t, :])
            last.then_inc(r.step, 1)
            dve.wait_ge(r.step, c + 1)
            dve.sem_inc(dve_passed, 1)
            for t in range(r.n):
                last = nc.vector.bn_aggr(r.mv[:, t, :], r.bn[:, t, :])
            last.then_inc(r.step, 1)

        def dve_guess(dve, r, c):
            dve.wait_ge(r.step, c)
            nc.vector.tensor_scalar(r.half[:, :], r.v[:, 0, :].bitcast(I32), 1, None,
                                    ALU.logical_shift_right).then_inc(r.step, 1)
            dve.wait_ge(r.step, c + 1)
            nc.vector.tensor_scalar(r.root[:, 0, :].bitcast(I32), r.half[:, :], -1.0, ROOT_GUESS, ALU.mult,
                                    ALU.add).then_inc(r.step, 1)

        def dve_newton(dve, r, c):
            y, yy, vyy = r.root[:, 0, :], r.root[:, 1, :], r.root[:, 2, :]
            dve.wait_ge(r.step, c)
            nc.vector.tensor_tensor(yy, y, y, ALU.mult).then_inc(r.step, 1)
            dve.wait_ge(r.step, c + 1)
            nc.vector.scalar_tensor_tensor(vyy, yy, -0.5, r.v[:, 0, :], ALU.mult, ALU.mult).then_inc(r.step, 1)
            dve.wait_ge(r.step, c + 2)
            nc.vector.scalar_tensor_tensor(y, vyy, 1.5, y, ALU.add, ALU.mult).then_inc(r.step, 1)

        def dve_ln(dve, r, x, c, piece):
            if piece == 0:
                dve_stats(dve, r, x, c)
                dve.wait_ge(r.step, c + 2)
                nc.vector.tensor_scalar(r.v[:, 0, :], r.mv[:, :, 1], LN_EPS, None, ALU.add).then_inc(r.step, 1)
                dve_guess(dve, r, c + 3)
            else:
                for k in range(3):
                    dve_newton(dve, r, c + 5 + 3 * k)
                dve.wait_ge(r.step, c + LN_STEPS)

        def dve_normed(r, x, dst):
            for t in range(NT):
                last = nc.vector.tensor_scalar(dst[:, t, :], x[:, t, :], r.mv[:, t, 0:1], r.root[:, 0, t:t + 1],
                                               ALU.subtract, ALU.mult)
            return last

        def turns(engine, turn):
            turn(-1, (1,))
            turn(0, (0, 1))
            with engine.Fori(1, B - 1) as b:
                turn(b, (-1, 0, 1))
            turn(B - 1, (-1, 0))
            turn(B, (-1,))

        def base_of(uses, b):
            def count(i, off):
                return sum((1, u[2], u[3])[i] for u in uses.values() if u[1] == off)

            base = []
            for i in range(3):
                before, own, after = count(i, 1), count(i, 0), count(i, -1)
                if isinstance(b, int) and b <= 0:
                    base.append(before * (b + 1))
                elif isinstance(b, int) and b == B:
                    base.append(B * (before + own) + (B - 1) * after)
                else:
                    base.append(b * (before + own + after) + (before - after))
            return base

        def use_of(uses, b, has, key):
            if key not in uses or uses[key][1] not in has:
                return None
            before = [u for k, u in uses.items() if k < key and u[1] in has]
            number, by_act, by_dve = base_of(uses, b)
            return (uses[key][0], uses[key][1], number + len(before), by_act + sum(u[2] for u in before),
                    by_dve + sum(u[3] for u in before))

        RAW = {"wq0": slice(0, 1024), "wk0": slice(1024, 2048), "wv0": slice(2048, 2560), "wo0": slice(2560, 3584)}
        SEQ1 = [("head", h) for h in range(12)] + [("slots", j) for j in range(PAIRS)] + \
               [("head", h) for h in range(12, H)]
        USES1 = {0: ("q1", 0, 1, 1), 1: ("k1", 0, 1, 1), 2: ("xT", 1, 1, 1), 3: ("v1", 0, 1, 1), 7: ("q0", 1, 1, 1),
                 8: ("rT", -1, 1, 1), 9: ("logit0", -1, 1, 0), 10: ("logit1", -1, 1, 0), 11: ("logit2", -1, 1, 0),
                 12: ("logit3", -1, 1, 0), 13: ("k0", 1, 1, 1), 14: ("v0", 1, 1, 1), 16: ("comb0", -1, 1, 0),
                 17: ("comb1", -1, 1, 0), 18: ("comb2", -1, 1, 0), 19: ("comb3", -1, 1, 0)}

        def unit1(b, n):
            if isinstance(b, int) and b <= 0:
                if b < 0 or n < 0 or SEQ1[n][0] == "slots":
                    return None
                return SEQ1[n] + (SEQ1[n][1],)
            kind, k = SEQ1[n % NU1]
            if isinstance(b, int) and b == B and n >= 0:
                return (kind, k, B * NU1 - PAIRS + k) if kind == "slots" else None
            return kind, k, b * NU1 - PAIRS + n

        def use1(b, has, n):
            use = use_of(USES1, b, has, n)
            return use and (use[0], use[1], use[2], use[4])

        def part1_pe(pe):
            w = u1
            pe.wait_ge(consts_made, 2)
            pe.wait_ge(slots_normed, 2)
            for j in range(PAIRS):
                if j > 1:
                    pe.wait_ge(snT_lo, j - 1)
                bank = halves(ps_s[:, j % 2, :])
                for c in range(DT):
                    for i in range(2):
                        last = nc.tensor.transpose(bank[:, c, i * P:i * P + P],
                                                   slot_raw[:, 2 * j + i, c * P:c * P + P], ident[:, :])
                last.then_inc(snT_ready, 1)
            pe.wait_ge(snT_lo, PAIRS)
            pe.wait_ge(w0_lo, 4)
            pe.wait_ge(consts_made, 4)

            def use_g(b, has, n):
                use = use1(b, has, n)
                if use is None:
                    return
                name, off, i, s = use
                pe.wait_ge(w.g_hi, since(i))
                pe.wait_ge(w.g_lo, since(s))
                kind, k = name[:-1], name[-1]
                if name == "xT":
                    pe.wait_ge(w.xn_made, b + off + 1)
                    last = pe_transposes(w.xn, ps_g)
                elif name == "rT":
                    pe.wait_ge(xr_made, b + off + 1)
                    last = pe_transposes(xr, ps_g)
                elif kind in ("q", "k"):
                    if kind == "k":
                        pe.wait_ge(w.ctx_lo_made, b + off + 1)
                    wt, src_hi, src_lo = (wq0, w.xT_hi, w.xT_lo) if kind == "q" else (wk0, w.ctxT_hi, w.ctxT_lo)
                    for i2 in range(2):
                        cols = slice((2 * int(k) + i2) * P, (2 * int(k) + i2 + 1) * P)
                        prods = [p for c in range(2) for p in terms(wt[:, 0, c, cols], wt[:, 1, c, cols],
                                                                    src_hi[:, c, :], src_lo[:, c, :])]
                        for m, (l, r) in enumerate(prods):
                            last = nc.tensor.matmul(halves(ps_g)[:, i2, :], l, r, start=m == 0, stop=m == 5)
                elif kind == "v":
                    cols = slice(int(k) * P, int(k) * P + P)
                    for t in range(NT):
                        tt = slice(t * P, t * P + P)
                        prods = [p for c in range(2) for p in terms(w.ctxT_hi[:, c, tt], w.ctxT_lo[:, c, tt],
                                                                    wv0[:, 0, c, cols], wv0[:, 1, c, cols])]
                        for m, (l, r) in enumerate(prods):
                            last = nc.tensor.matmul(ps_g[:, t * P:t * P + P], l, r, start=m == 0, stop=m == 5)
                elif kind == "logit":
                    t, half = int(k) % 2, int(k) // 2
                    tt, m = slice(t * P, t * P + P), slice(half * 512, half * 512 + 512)
                    prods = [p for c in range(DT) for p in terms(rT_hi[:, c, tt], rT_lo[:, c, tt],
                                                                 snT[:, 0, c, m], snT[:, 1, c, m])]
                    for m, (l, r) in enumerate(prods):
                        last = nc.tensor.matmul(ps_g, l, r, start=m == 0, stop=m == 5)
                else:
                    pe.wait_ge(comb_ready, (b + off) * NT + NT)
                    for i2 in range(2):
                        for t in range(NT):
                            m = (2 * int(k) + i2) * P
                            last = nc.tensor.transpose(halves(ps_g)[:, i2, t * P:t * P + P],
                                                       comb[:, t, m:m + P], ident[:, :])
                last.then_inc(w.g_ready, 1)

            def scores(b, has, n):
                kind, k, u = unit1(b, n)
                pe.wait_ge(w.exp_ready, since(u - 1))
                bank = halves(ps_s[:, n % 2, :])
                if kind == "head":
                    g, r = k // GH, 32 * (k % GH)
                    if k == 0:
                        pe.wait_ge(w.g_lo, base_of(USES1, b)[2])
                    if k == 2 * GH:
                        pe.wait_ge(w.g_lo, use1(b, has, 1)[3] + 1)
                    if k % (2 * GH) == 0:
                        pe.wait_ge(mask_made, b * 2 + 1 + k // (2 * GH))
                    for q in range(NT):
                        lhs = q_mix[r:r + 32, g, q * P:q * P + P]
                        nc.tensor.matmul(bank[:, q, :], lhs, k_hi[r:r + 32, g, :], start=True, stop=False)
                        nc.tensor.matmul(bank[:, q, :], lhs, k_lo[r:r + 32, g, :], start=False, stop=False)
                        last = nc.tensor.matmul(bank[:, q, :], ones[r:r + 1, :], mask_bias[r:r + 1, k // (2 * GH), :],
                                                start=False, stop=True)
                else:
                    pe.wait_ge(w.g_hi, use1(b, has, 10 if k < PAIRS // 2 else 12)[2] + 1)
                    for i in range(2):
                        for t in range(NT):
                            m = (2 * k + i) * P
                            last = nc.tensor.transpose(bank[:, i, t * P:t * P + P], logit[:, t, m:m + P], ident[:, :])
                last.then_inc(w.scores_ready, 1)

            def product(b, has, n):
                kind, k, u = unit1(b, n)
                hb = b - 1 if n < 0 else b
                m = n % 4
                pe.wait_ge(w.prob_lo_ready, since(u + 1))
                if kind == "head":
                    g = k // GH
                    if k % GH == 0:
                        if g in (0, 3):
                            pe.wait_ge(slot_copied, hb * PAIRS + g)
                        if g == 1:
                            pe.wait_ge(w.oT_lo_ready, hb * G)
                        elif g > 1:
                            pe.wait_ge(w.oT_lo_ready, hb * G + g - 1)
                    if k == 0:
                        pe.wait_ge(w.g_lo, base_of(USES1, b)[2])
                    if k == 2 * GH:
                        pe.wait_ge(w.g_lo, use1(b, has, 3)[3] + 1)
                    col = (k % GH) * P
                    for t in range(NT):
                        for i, pr in enumerate((w.prob_hi, w.prob_lo)):
                            last = nc.tensor.matmul(ps_o[:, g % 2, 0:N], v_pad[:, t, g, col:col + P], pr[:, m % 2, t, :],
                                                    start=k % GH == 0 and t == 0 and i == 0,
                                                    stop=k % GH == GH - 1 and t == NT - 1 and i == 1)
                else:
                    if k < 2 and 0 in has:
                        pe.wait_ge(w.oT_lo_ready, b * G + k + 2)
                    elif k < 2:
                        pe.wait_ge(w.oT_lo_ready, B * G)
                        pe.wait_ge(slot_copied, B * PAIRS)
                    else:
                        pe.wait_ge(slot_copied, b * PAIRS + k - 1)
                    pe.wait_ge(xr_hi_made, b)
                    pe.wait_ge(xr_lo_made, b)
                    for d in range(DT):
                        dd = slice(d * P, d * P + P)
                        prods = [p for t in range(NT) for p in terms(xr_hi[:, t, dd], xr_lo[:, t, dd],
                                                                     w.prob_hi[:, m % 2, t, :],
                                                                     w.prob_lo[:, m % 2, t, :])]
                        for i, (l, r) in enumerate(prods):
                            last = nc.tensor.matmul(halves(ps_o[:, (k + 1) % 2, :])[:, d, :], l, r,
                                                    start=i == 0, stop=i == 5)
                last.then_inc(w.pv_done, 1)

            def turn(b, has):
                for n in range(NU1):
                    if unit1(b, n):
                        scores(b, has, n)
                    if n >= 16:
                        use_g(b, has, n)
                    if unit1(b, n - 2):
                        pe_unit_transposes(pe, w, unit1(b, n - 2)[2], (n - 2) % 4)
                    if n in (9, 13, 17) and 0 in has:
                        pe_out_proj(pe, w, b, (n - 9) // 4, G, wo0)
                    if n == 5 and -1 in has:
                        pe_out_proj(pe, w, b - 1, 3, G, wo0)
                    if unit1(b, n - 4):
                        product(b, has, n - 4)
                    if n < 16:
                        use_g(b, has, n)

            turns(pe, turn)

        def part1_act(act):
            w = u1
            for j in range(PAIRS):
                act.wait_ge(snT_ready, j + 1)
                nc.scalar.activation(snT[:, 0, :, j * N:j * N + N], halves(ps_s[:, j % 2, :]),
                                     ACT.Copy).then_inc(snT_hi, 1)
            act.wait_ge(consts_made, 4)

            def copy_g(b, has, n):
                use = use1(b, has, n)
                if use is None:
                    return
                name, off, i, s = use
                act.wait_ge(w.g_ready, i + 1)
                kind, k = name[:-1], name[-1]
                if name == "xT":
                    nc.scalar.activation(w.xT_hi[:, :, :], halves(ps_g), ACT.Copy).then_inc(w.g_hi, 1)
                elif name == "rT":
                    nc.scalar.activation(rT_hi[:, :, :], halves(ps_g), ACT.Copy).then_inc(w.g_hi, 1)
                elif kind == "q":
                    act.wait_ge(w.g_lo, since(s))
                    nc.scalar.activation(q_full[:, :, :], halves(ps_g), ACT.Copy).then_inc(w.g_hi, 1)
                elif kind == "k":
                    j = int(k)
                    act.wait_ge(w.scores_ready, since(units_of_half(b, j)))
                    nc.scalar.activation(k_hi[:, 2 * j:2 * j + 2, :], halves(ps_g), ACT.Copy).then_inc(w.g_hi, 1)
                elif kind == "v":
                    j = int(k)
                    act.wait_ge(w.pv_done, since(units_of_half(b, j)))
                    vv = v_pad[:, :, 2 * j:2 * j + 2, :].rearrange("p t g (j w) -> p t (g j) w", w=VW)
                    for t in range(NT):
                        last = nc.scalar.activation(vv[:, t, :, 0:HD0],
                                                    ps_g[:, t * P:t * P + P].rearrange("p (j d) -> p j d", d=HD0),
                                                    ACT.Copy)
                    last.then_inc(w.g_hi, 1)
                elif kind == "logit":
                    t, half = int(k) % 2, int(k) // 2
                    act.wait_ge(cexp_ready, (b + off) * NT)
                    act.wait_ge(w.scores_ready, b * NU1 - PAIRS)
                    nc.scalar.activation(logit[:, t, half * 512:half * 512 + 512], ps_g, ACT.Copy).then_inc(w.g_hi, 1)
                else:
                    act.wait_ge(comb_stored, (b + off) * 16)
                    nc.scalar.activation(combT[:, 2 * int(k):2 * int(k) + 2, :], halves(ps_g),
                                         ACT.Copy).then_inc(w.g_hi, 1)

            def store_slots(b, j):
                act.wait_ge(slot_copied, b * PAIRS + j + 1)
                for d in range(DT):
                    act.dma_start(slots_dram[2 * j:2 * j + 2, :, d, b - 1, :].rearrange("e p s -> p e s"),
                                  slot_out[:, j, d, :].rearrange("p (e s) -> p e s", e=2)).then_inc(slots_stored, 16)

            def turn(b, has):
                for n in range(NU1):
                    if unit1(b, n - 3):
                        act_unit_hi(act, w, unit1(b, n - 3)[2], (n - 3) % 4)
                    if n in (8, 12, 16) and 0 in has:
                        copy_heads(b, n // 4 - 2)
                    if n == 4 and -1 in has:
                        copy_heads(b - 1, 3)
                    if n <= 16:
                        copy_g(b, has, n - 1)
                    if unit1(b, n):
                        act_unit_exp(act, w, unit1(b, n)[2], n % 4)
                    if n == 5 and 1 in has:
                        act.wait_ge(w.ctx_loaded, b * 16 + 32)
                        if 0 in has:
                            act.wait_ge(w.g_ready, use1(b, has, 3)[2] + 1)
                        nc.scalar.activation(w.ctxT_hi[:, :, :], w.ctxT[:, :, :], ACT.Copy).then_inc(w.ctx_hi_made, 1)
                    if n == 9 and -1 in has:
                        act.wait_ge(xr_made, b)
                        act.wait_ge(w.pv_done, since(b * NU1 - 2 * PAIRS))
                        nc.scalar.activation(xr_hi[:, :, :], xr[:, :, :], ACT.Copy).then_inc(xr_hi_made, 1)
                    if n in (13, 14) and -1 in has:
                        t = n - 13
                        act.wait_ge(cmax_ready, (b - 1) * NT + t + 1)
                        act.wait_ge(cinv_ready, (b - 1) * NT)
                        act.wait_ge(w.g_ready, use1(b, has, 9)[2])
                        nc.scalar.activation(comb[:, t, :], logit[:, t, :], ACT.Exp, bias=comb_stat[:, 0, t:t + 1],
                                             accum_out=comb_stat[:, 1, t:t + 1]).then_inc(cexp_ready, 1)
                    if n >= 16:
                        copy_g(b, has, n)
                    if n in (18, 19) and -1 in has:
                        store_slots(b, n - 18)
                if -1 in has:
                    store_slots(b, 2)
                    store_slots(b, 3)
                    act.wait_ge(w.g_hi, use1(b, has, 19)[2] + 1)
                    act.dma_start(comb_dram[b - 1, :, :, :], combT[:, :, :]).then_inc(comb_stored, 16)

            def copy_heads(b, g):
                act.wait_ge(w.pv_done, since(units_of_group(b, g)))
                act.wait_ge(w.oproj_done, since(b * G + g - 1))
                nc.scalar.activation(w.oT_hi[:, g % 2, :], ps_o[:, g % 2, 0:N], ACT.Copy).then_inc(w.oT_hi_ready, 1)

            turns(act, turn)
            act.wait_ge(comb_stored, 16 * B)
            act.wait_ge(slots_stored, 16 * B * PAIRS * DT)

        def units_of_half(b, j):
            if j == 1 or (isinstance(b, int) and b < 0):
                return b * NU1 - PAIRS
            return b * NU1 + 2 * GH - (PAIRS if not isinstance(b, int) or b else 0)

        def units_of_group(b, g):
            if isinstance(b, int) and b == 0:
                return g * GH + GH
            return b * NU1 + g * GH + GH - (0 if g == G - 1 else PAIRS)

        def part1_dve(dve):
            w = u1
            r = slot_norm
            dve.wait_ge(slots_loaded, 16)
            dve_stats(dve, r, slot_raw, 0)
            dve.wait_ge(r.step, 2)
            nc.vector.tensor_tensor(r.v[:, 1, :], r.mv[:, :, 0], r.mv[:, :, 0], ALU.mult).then_inc(r.step, 1)
            dve.wait_ge(r.step, 3)
            nc.vector.tensor_tensor(r.v[:, 1, :], r.v[:, 1, :], r.mv[:, :, 1], ALU.add).then_inc(r.step, 1)
            dve.wait_ge(r.step, 4)
            nc.vector.tensor_scalar(r.v[:, 0, :], r.v[:, 1, :], RMS_FLOOR / D, None, ALU.max).then_inc(r.step, 1)
            dve_guess(dve, r, 5)
            for k in range(3):
                dve_newton(dve, r, 7 + 3 * k)
            dve.wait_ge(r.step, 16)
            for e in range(E):
                last = nc.vector.tensor_scalar(slot_raw[:, e, :], slot_raw[:, e, :], r.root[:, 0, e:e + 1], None,
                                               ALU.mult)
            last.then_inc(slots_normed, 1)
            dve.wait_ge(slots_normed, 1)
            dve.wait_ge(small_loaded, 64)
            nc.vector.tensor_tensor(slot_raw[:, :, :], slot_raw[:, :, :],
                                    gamma_s[:, :].unsqueeze(1).to_broadcast([P, E, D]), ALU.mult).then_inc(slots_normed, 1)
            for i, (name, wt, kp, scale, loaded) in enumerate((("wq0", wq0, P, HD0 ** -0.5, wq0_loaded),
                                                               ("wk0", wk0, KC, 1.0, wk0_loaded),
                                                               ("wv0", wv0, KC, 1.0, wv0_loaded),
                                                               ("wo0", wo0, P, 1.0, wo0_loaded))):
                full = raw0[0:kp, RAW[name]]
                hi = wt[:, 0, :, :].rearrange("p c n -> p (c n)")
                lo = wt[:, 1, :, :].rearrange("p c n -> p (c n)")
                dve.wait_ge(loaded, 16)
                nc.vector.tensor_scalar(hi, full, scale, None, ALU.mult).then_inc(w0_hi, 1)
                dve.wait_ge(w0_hi, i + 1)
                nc.vector.scalar_tensor_tensor(lo, full, scale, hi.bitcast(F32), ALU.mult,
                                               ALU.subtract).then_inc(w0_lo, 1)
            for j in range(PAIRS):
                dve.wait_ge(snT_hi, j + 1)
                dve_lo(snT[:, 1, :, j * N:j * N + N], halves(ps_s[:, j % 2, :]),
                       snT[:, 0, :, j * N:j * N + N]).then_inc(snT_lo, 1)

            def copy_g(b, has, n):
                use = use1(b, has, n)
                if use is None or not USES1[n][3]:
                    return
                name, off, i, s = use
                dve.wait_ge(w.g_hi, i + 1)
                kind, k = name[:-1], name[-1]
                if name == "xT":
                    dve_lo(w.xT_lo[:, :, :], halves(ps_g), w.xT_hi[:, :, :]).then_inc(w.g_lo, 1)
                elif name == "rT":
                    dve_lo(rT_lo[:, :, :], halves(ps_g), rT_hi[:, :, :]).then_inc(w.g_lo, 1)
                elif kind == "q":
                    j = int(k)
                    dve.wait_ge(w.scores_ready, since(units_of_half(b, j)))
                    qf = q_full[:, :, :].rearrange("p a n -> p (a n)").bitcast(F32)
                    nc.vector.scalar_tensor_tensor(q_mix[:, 2 * j:2 * j + 2, :].rearrange("p a n -> p (a n)"), qf,
                                                   lo_rows[:, 0:1], ps_g, ALU.mult, ALU.add).then_inc(w.g_lo, 1)
                elif kind == "k":
                    j = int(k)
                    dve_lo(k_lo[:, 2 * j:2 * j + 2, :], halves(ps_g), k_hi[:, 2 * j:2 * j + 2, :]).then_inc(w.g_lo, 1)
                else:
                    j = int(k)
                    vv = v_pad[:, :, 2 * j:2 * j + 2, :].rearrange("p t g (j w) -> p t (g j) w", w=VW)
                    for t in range(NT):
                        last = dve_lo(vv[:, t, :, HD0:2 * HD0],
                                      ps_g[:, t * P:t * P + P].rearrange("p (j d) -> p j d", d=HD0), vv[:, t, :, 0:HD0])
                    last.then_inc(w.g_lo, 1)

            def make_mask(b, turn_b, j):
                dve.wait_ge(w.scores_ready, since(units_of_half(turn_b, j)))
                nc.vector.tensor_scalar(mask_bias[:, j, :], mask_u8[:, b, :], -1.0, MASKED, ALU.add,
                                        ALU.mult).then_inc(mask_made, 1)

            def copy_heads(b, g):
                dve.wait_ge(w.oT_hi_ready, b * G + g + 1)
                dve_lo(w.oT_lo[:, g % 2, :], ps_o[:, g % 2, 0:N], w.oT_hi[:, g % 2, :]).then_inc(w.oT_lo_ready, 1)

            def copy_slots(b, j):
                dve.wait_ge(w.pv_done, b * NU1 + 2 * GH + j + 1 if not isinstance(b, int) or b < B else B * NU1 - PAIRS + j + 1)
                dve.wait_ge(slots_stored, (b - 1) * 16 * PAIRS * DT)
                nc.vector.tensor_copy(slot_out[:, j, :, :], halves(ps_o[:, (j + 1) % 2, :])).then_inc(slot_copied, 1)

            def turn(b, has):
                for n in range(NU1):
                    if unit1(b, n):
                        dve_unit_max(dve, w, unit1(b, n)[2], n % 4)
                    if unit1(b, n - 1):
                        dve_unit_inv(dve, w, unit1(b, n - 1)[2], (n - 1) % 4)
                    if n in (17, 18, 19) and -1 in has:
                        copy_slots(b, n - 17)
                    if unit1(b, n - 3):
                        dve_unit_lo(dve, w, unit1(b, n - 3)[2], (n - 3) % 4)
                    if n in (8, 12, 16) and 0 in has:
                        copy_heads(b, n // 4 - 2)
                    if n == 4 and -1 in has:
                        copy_heads(b - 1, 3)
                    if n <= 15:
                        copy_g(b, has, n - 1)
                    if n == 0 and 1 in has:
                        dve.wait_ge(w.x_loaded, b * 16 + 32)
                        dve_ln(dve, x_norm, w.x_in, (b + 1) * LN_STEPS, 0)
                    if n == 2 and 0 in has:
                        make_mask(b, b, 1)
                    if n == 9 and 1 in has:
                        make_mask(b + 1, b, 0)
                    if n == 1 and 1 in has:
                        dve_ln(dve, x_norm, w.x_in, (b + 1) * LN_STEPS, 1)
                        if 0 in has:
                            dve.wait_ge(w.g_lo, use1(b, has, 0)[3])
                        dve_normed(x_norm, w.x_in, w.xn).then_inc(w.xn_made, 1)
                    if n == 5 and -1 in has:
                        dve.wait_ge(w.oproj_done, b * G)
                        dve.wait_ge(res_loaded, b * 16)
                        dve.wait_ge(x1_stored, b * 16 - 16)
                        nc.vector.tensor_tensor(x1[:, :, :], halves(ps_y), x_res[:, :, :], ALU.add).then_inc(w.sum_taken, 1)
                        dve.wait_ge(w.sum_taken, b)
                        dve_stats(dve, r_norm, x1, (b - 1) * RMS_STEPS)
                    if n == 6 and -1 in has:
                        r, c = r_norm, (b - 1) * RMS_STEPS
                        dve.wait_ge(r.step, c + 2)
                        nc.vector.tensor_scalar(r.v[:, 1, :], r.mv[:, :, 1], LN_EPS, RMS_FLOOR / D, ALU.add,
                                                ALU.mult).then_inc(r.step, 1)
                        dve.wait_ge(r.step, c + 3)
                        nc.vector.tensor_tensor(r.v[:, 0, :], r.v[:, 1, :], r.mv[:, :, 1], ALU.max).then_inc(r.step, 1)
                        dve_guess(dve, r, c + 4)
                        dve_newton(dve, r, c + 6)
                    if n == 7 and -1 in has:
                        r, c = r_norm, (b - 1) * RMS_STEPS
                        dve_newton(dve, r, c + 9)
                        dve_newton(dve, r, c + 12)
                        dve.wait_ge(r.step, c + 15)
                        dve.wait_ge(xr_made, b - 1)
                        dve_normed(r, x1, xc).then_inc(xc_made, 1)
                    if n in (12, 13) and -1 in has:
                        t = n - 12
                        dve.wait_ge(w.g_hi, use1(b, has, 11 + t)[2] + 1)
                        nc.vector.tensor_reduce(comb_stat[:, 0, t:t + 1], logit[:, t, :], AX.X, ALU.max,
                                                negate=True).then_inc(cmax_ready, 1)
                    if n == 15 and -1 in has:
                        for t in range(NT):
                            dve.wait_ge(cexp_ready, (b - 1) * NT + t + 1)
                            nc.vector.reciprocal(comb_stat[:, 2, t:t + 1], comb_stat[:, 1, t:t + 1]).then_inc(cinv_ready, 1)
                        for t in range(NT):
                            dve.wait_ge(cinv_ready, (b - 1) * NT + t + 1)
                            nc.vector.tensor_scalar(comb[:, t, :], comb[:, t, :], comb_stat[:, 2, t:t + 1], None,
                                                    ALU.mult).then_inc(comb_ready, 1)
                if isinstance(b, int) and b == 0:
                    dve.sem_inc(slot_copied, PAIRS)
                if -1 in has:
                    copy_slots(b, 3)

            turns(dve, turn)

        def part1_pool(pool):
            w = u1
            nc.gpsimd.memset(ident[:, :], 0.0).then_inc(consts_made, 1)
            pool.wait_ge(consts_made, 1)
            nc.gpsimd.affine_select(out=ident[:, :], in_=ident[:, :], compare_op=ALU.not_equal, fill=1.0, base=0,
                                    pattern=[[-1, P]], channel_multiplier=1).then_inc(consts_made, 1)
            nc.gpsimd.memset(ones[:, :].bitcast(F32), 1.0).then_inc(consts_made, 1)
            nc.gpsimd.memset(v_pad[:, :, :, :].rearrange("p t g w -> p (t g w)").bitcast(F32),
                             0.0).then_inc(consts_made, 1)
            pool.wait_ge(small_loaded, 64)

            def turn(b, has):
                for n in range(NU1):
                    if unit1(b, n - 1):
                        pool_unit_norm(pool, w, unit1(b, n - 1)[2], (n - 1) % 4)
                    if n == 5 and 1 in has:
                        pool.wait_ge(w.ctx_hi_made, b + 2)
                        nc.gpsimd.tensor_tensor(w.ctxT_lo[:, :, :], w.ctxT[:, :, :], w.ctxT_hi[:, :, :].bitcast(F32),
                                                ALU.subtract).then_inc(w.ctx_lo_made, 1)
                    if n == 7 and -1 in has:
                        pool.wait_ge(xc_made, b)
                        pool.wait_ge(xr_lo_made, b - 1)
                        pool.wait_ge(w.g_ready, base_of(USES1, b)[0])
                        nc.gpsimd.tensor_tensor(xr[:, :, :], xc[:, :, :],
                                                gamma[:, :].unsqueeze(1).to_broadcast([P, NT, D]),
                                                ALU.mult).then_inc(xr_made, 1)
                    if n == 10 and -1 in has:
                        pool.wait_ge(xr_hi_made, b)
                        nc.gpsimd.tensor_tensor(xr_lo[:, :, :], xr[:, :, :], xr_hi[:, :, :].bitcast(F32),
                                                ALU.subtract).then_inc(xr_lo_made, 1)

            turns(pool, turn)

        def part1_sp(sp):
            w = u1
            sp.dma_start(slot_raw[:, :, :], a["slots"].rearrange("e s d -> s e d")).then_inc(slots_loaded, 16)
            sp.dma_start(gamma_s[:, :], a["gamma_s"].partition_broadcast(P)).then_inc(small_loaded, 16)
            sp.dma_start(mask_u8[:, :, :].rearrange("p b n -> p (b n)"), a["mask"].rearrange("b n -> (b n)").partition_broadcast(P)).then_inc(small_loaded, 16)
            for name, kp, src, loaded in (("wq0", P, a["Wq0"], wq0_loaded), ("wk0", KC, a["Wk0"], wk0_loaded),
                                          ("wv0", KC, a["Wv0"], wv0_loaded)):
                sp.dma_start(raw0[0:kp, RAW[name]].rearrange("p (c n) -> p c n", c=2),
                             src.rearrange("(c p) n -> p c n", c=2)).then_inc(loaded, 16)
            sp.dma_start(raw0[:, RAW["wo0"]].rearrange("p (g n) -> p g n", g=G), a["Wo0"]).then_inc(wo0_loaded, 16)
            sp.dma_start(gamma[:, :], a["gamma"].partition_broadcast(P)).then_inc(small_loaded, 16)
            sp.dma_start(lo_rows[:, :], a["lo_rows"]).then_inc(small_loaded, 16)

            def turn(b, has):
                if 1 in has:
                    sp.wait_ge(w.xn_made, b + 1)
                    sp.sem_inc(sp_passed, 1)
                    sp.dma_start(w.x_in[:, :, :], a["x"][b + 1, :, :].rearrange("(t p) d -> p t d", p=P)).then_inc(w.x_loaded, 16)
                    sp.wait_ge(w.ctx_lo_made, b + 1)
                    sp.sem_inc(sp_passed, 1)
                    sp.dma_start(w.ctxT[:, :, :],
                                 a["ctxT"][b + 1, :, :].rearrange("(c p) n -> p c n", c=2)).then_inc(w.ctx_loaded, 16)
                if -1 in has:
                    sp.wait_ge(w.sum_taken, b)
                    sp.sem_inc(sp_passed, 1)
                    sp.dma_start(x1_dram[b - 1, :, :, :], x1[:, :, :]).then_inc(x1_stored, 16)
                if 0 in has:
                    sp.wait_ge(w.sum_taken, b)
                    sp.sem_inc(sp_passed, 1)
                    sp.dma_start(x_res[:, :, :], a["x"][b, :, :].rearrange("(t p) d -> p t d", p=P)).then_inc(res_loaded, 16)

            turns(sp, turn)
            sp.wait_ge(x1_stored, 16 * B)

        def split_pieces():
            def w1_piece(i):
                cols = slice(i * 2 * P, (i + 1) * 2 * P)
                return w1_raw[:, :, cols], w1_s[:, 0, :, cols], w1_s[:, 1, :, cols]

            def w2_piece(i):
                rows = slice(2 * i, 2 * i + 2)
                return w2_raw[:, rows, :], w2_s[:, 0, rows, :], w2_s[:, 1, rows, :]

            def sl_piece(i):
                cols = slice(i * 512, i * 512 + 512)
                return sl_raw[:, :, cols], sl_s[:, 0, :, cols], sl_s[:, 1, :, cols]

            pieces = [(sl_loaded, sl_piece(0))]
            for i in range(4):
                pieces += [(w1_loaded, w1_piece(i)), (w2_loaded, w2_piece(i))]
            return pieces + [(sl_loaded, sl_piece(1))]

        PIECES = split_pieces()
        h_banks = [ps_s[:, 0, :], ps_s[:, 1, :], ps_t[:, 0, :], ps_t[:, 1, :]]
        eo_banks = [ps_o, ps_yg]

        def part2_pe(pe):
            with pe.Fori(0, E) as e:
                for n in range(HU + 2):
                    if n < HU:
                        half, hc = n // HT, n % HT
                        if n == 0:
                            pe.wait_ge(e_lo_dve, at(e, 2, 2))
                        elif n < HT and n % 2 == 0:
                            pe.wait_ge(e_lo_pool, at(e, 8, n))
                        elif n == HT:
                            pe.wait_ge(e_lo_pool, at(e, 8, 8))
                        pe.wait_ge(gelu_done, at(e, HU, n - 3))
                        cols, m = slice(hc * P, hc * P + P), slice(half * 512, half * 512 + 512)
                        prods = [p for c in range(DT) for p in terms(w1_s[:, 0, c, cols], w1_s[:, 1, c, cols],
                                                                     sl_s[:, 0, c, m], sl_s[:, 1, c, m])]
                        for k, (l, r) in enumerate(prods):
                            last = nc.tensor.matmul(h_banks[n % 4], l, r, start=k == 0, stop=k == 5)
                        last.then_inc(h_ready, 1)
                    if n >= 2:
                        u = n - 2
                        half, hc = u // HT, u % HT
                        pe.wait_ge(h_lo_made, at(e, HU, u + 1))
                        if hc % 2 == 0 and half == 0:
                            pe.wait_ge(e_lo_pool, at(e, 8, hc + 1))
                        if hc == 0:
                            pe.wait_ge(eo_made, at(e, 4, 0))
                        for i in range(BH):
                            ss = slice(i * S, i * S + S)
                            for k, (l, r) in enumerate(terms(h_hi[:, u % 4, ss], h_lo[:, u % 4, ss],
                                                             w2_s[:, 0, hc, :], w2_s[:, 1, hc, :])):
                                last = nc.tensor.matmul(halves(eo_banks[half][:, i // 2, :])[:, i % 2, :], l, r,
                                                        start=hc == 0 and i % 2 == 0 and k == 0,
                                                        stop=hc == HT - 1 and k == 2, skip_group_check=True)
                        last.then_inc(eo_part, 1)

        def part2_act(act):
            def split_hi(e, i):
                loaded, (full, hi, _) = PIECES[i]
                act.wait_ge(loaded, at(e, 16, 16))
                act.wait_ge(h_ready, at(e, HU, 0))
                act.wait_ge(eo_part, at(e, HU, 0))
                nc.scalar.activation(hi, full, ACT.Copy).then_inc(e_hi, 1)

            with act.Fori(0, E) as e:
                for i in range(3):
                    split_hi(e, i)
                for n in range(HU):
                    if n == 0:
                        act.wait_ge(b_loaded, at(e, 32, 32))
                    act.wait_ge(h_ready, at(e, HU, n + 1))
                    act.wait_ge(h_lo_made, at(e, HU, n - 1))
                    nc.scalar.activation(h_raw[:, n % 2, :], h_banks[n % 4], ACT.Gelu,
                                         bias=b1_sb[:, n % HT:n % HT + 1]).then_inc(gelu_done, 1)
                    if n + 3 < NSPLIT:
                        split_hi(e, n + 3)
                for half in range(2):
                    act.wait_ge(eo_made, at(e, 4, 2 * half + 2))
                    act.dma_start(eo_dram_of(e)[:, half * BH:half * BH + BH, :],
                                  eo[:, half, :, :, :].rearrange("p a i d -> p (a i) d")).then_inc(eo_stored, 16)
            act.wait_ge(eo_stored, 16 * 2 * E)

        def eo_dram_of(e):
            return eo_dram[e, :, :, :]

        def part2_dve(dve):
            with dve.Fori(0, E) as e:
                for i in range(2):
                    _, (full, hi, lo) = PIECES[i]
                    dve.wait_ge(e_hi, at(e, NSPLIT, i + 1))
                    dve_lo(lo, full, hi).then_inc(e_lo_dve, 1)
                for n in range(HU + 3):
                    if n < HU:
                        dve.wait_ge(gelu_done, at(e, HU, n + 1))
                        dve.wait_ge(eo_part, at(e, HU, n - 3))
                        nc.vector.tensor_copy(h_hi[:, n % 4, :], h_raw[:, n % 2, :]).then_inc(h_hi_made, 1)
                        dve.wait_ge(h_hi_made, at(e, HU, n + 1))
                        dve_lo(h_lo[:, n % 4, :], h_raw[:, n % 2, :], h_hi[:, n % 4, :]).then_inc(h_lo_made, 1)
                    if n in (HT + 2, HU + 2):
                        half = (n - 2) // HT - 1
                        dve.wait_ge(eo_part, at(e, HU, HT * (half + 1)))
                        dve.wait_ge(eo_stored, at(e, 32, 0))
                        dve.wait_ge(b_loaded, at(e, 32, 32))
                        for i in range(2):
                            nc.vector.tensor_tensor(eo[:, half, i, :, :], halves(eo_banks[half][:, i, :]),
                                                    b2_sb[:, :].unsqueeze(1).to_broadcast([P, 2, D]),
                                                    ALU.add).then_inc(eo_made, 1)

        def part2_pool(pool):
            with pool.Fori(0, E) as e:
                for i in range(2, NSPLIT):
                    _, (full, hi, lo) = PIECES[i]
                    pool.wait_ge(e_hi, at(e, NSPLIT, i + 1))
                    nc.gpsimd.tensor_tensor(lo, full, hi.bitcast(F32), ALU.subtract).then_inc(e_lo_pool, 1)

        def part2_sp(sp):
            with sp.Fori(0, E) as e:
                sp.wait_ge(e_lo_pool, at(e, 8, 0))
                sp.sem_inc(sp_passed, 1)
                sp.wait_ge(e_lo_dve, at(e, 2, 0))
                sp.sem_inc(sp_passed, 1)
                sp.dma_start(sl_raw[:, :, :], slots_dram[e, :, :, :, :].rearrange("p t b s -> p t (b s)")).then_inc(sl_loaded, 16)
                sp.dma_start(w1_raw[:, :, :], a["w1"][e, :, :].rearrange("(c p) n -> p c n", p=P)).then_inc(w1_loaded, 16)
                sp.dma_start(w2_raw[:, :, :], a["w2"][e, :, :].rearrange("(h p) n -> p h n", p=P)).then_inc(w2_loaded, 16)
                sp.wait_ge(eo_made, at(e, 4, 0))
                sp.sem_inc(sp_passed, 1)
                sp.wait_ge(gelu_done, at(e, HU, 0))
                sp.sem_inc(sp_passed, 1)
                sp.dma_start(b1_sb[:, :], a["b1"][e, :, :]).then_inc(b_loaded, 16)
                sp.dma_start(b2_sb[:, :], a["b2"][e, :].partition_broadcast(P)).then_inc(b_loaded, 16)

        comb_flat = comb_raw[:, :, :].rearrange("p e n -> p (e n)")
        eo_flat = eo_raw[:, :, :].rearrange("p e n -> p (e n)")
        W3 = ((wq1[:, :, :, :].rearrange("p s c n -> p s (c n)"), comb_flat, P, 2,
               a["w_q"].rearrange("(c p) n -> p c n", c=2), HD1 ** -0.5),
              (wk1[:, :, :, :].rearrange("p s c n -> p s (c n)"), eo_flat, KC, 2,
               a["w_k"].rearrange("(c p) n -> p c n", c=2), 1.0),
              (wv1[:, :, :, :].rearrange("p s c n -> p s (c n)"), comb_flat, KC, 2,
               a["w_v"].rearrange("(c p) n -> p c n", c=2), 1.0),
              (wo1[:, :, :, :].rearrange("p s c n -> p s (c n)"), eo_flat, P, HP,
               a["w_out"].rearrange("(c p) n -> p c n", c=HP), 1.0),
              (wf[:, :, :, :, :].rearrange("p s i c n -> p s (i c n)"), comb_flat, P, 6,
               a["wf"].rearrange("i (c p) n -> p (i c) n", c=2), 1.0))
        USES3 = {(2 * p - 4, 1): (f"pair{p}", 0, 1, 1) for p in range(2, HP)} | {
            (1, 1): ("experts0", 1, 0, 1), (3, 1): ("v2", 0, 1, 1), (5, 1): ("experts1", 1, 0, 1),
            (7, 1): ("shift", -1, 1, 0), (9, 1): ("v3", 0, 1, 1), (11, 0): ("xT", 1, 1, 1),
            (11, 1): ("mix_k", -1, 1, 0), (12, 0): ("mix_r", -1, 0, 1), (12, 1): ("pair0", 1, 1, 1),
            (13, 1): ("v0", 1, 1, 1), (14, 0): ("mix_v", -1, 0, 1), (14, 1): ("pair1", 1, 1, 1),
            (15, 0): ("v1", 1, 1, 1)}

        def unit3(b, n):
            if isinstance(b, int) and ((b <= 0 and n < 0) or b < 0 or (b == B and n >= 0)):
                return None
            return b * H + n

        def pair_of(n):
            return ((n - 6) // 2, 0) if n >= 6 else ((n + H - 6) // 2, -1)

        def has_pair(b, off):
            return not isinstance(b, int) or 0 <= b + off < B

        def part3_pe(pe):
            w = u3
            pe.wait_ge(w3_lo, len(W3))
            pe.wait_ge(tables_made, 3)

            def use_g(b, has, key):
                use = use_of(USES3, b, has, key)
                if use is None:
                    return
                name, off, _, by_act, by_dve = use
                pe.wait_ge(w.g_hi, by_act)
                pe.wait_ge(w.g_lo, by_dve)
                nb = b + off
                if name[:7] == "experts":
                    half = int(name[7])
                    pe.wait_ge(cs_lo, nb * PAIRS + 2 * half + 2)
                    pe.wait_ge(es_lo, nb * PAIRS + 2 * half + 2)
                    for t in range(NT):
                        tt = slice(t * P, t * P + P)
                        for e in range(E // 2):
                            for k, (l, r) in enumerate(terms(comb_s[:, 0, e, tt], comb_s[:, 1, e, tt],
                                                             eo_s[:, 0, e, :], eo_s[:, 1, e, :])):
                                last = nc.tensor.matmul(halves(ps_g)[:, t, :], l, r, start=e == 0 and k == 0,
                                                        stop=e == E // 2 - 1 and k == 2)
                elif name[0] == "v":
                    t, half = int(name[1]) % 2, int(name[1]) // 2
                    pe.wait_ge(w.ctx_lo_made, nb + 1)
                    tt, m = slice(t * P, t * P + P), slice(half * 512, half * 512 + 512)
                    prods = [p for c in range(2) for p in terms(w.ctxT_hi[:, c, tt], w.ctxT_lo[:, c, tt],
                                                                wv1[:, 0, c, m], wv1[:, 1, c, m])]
                    for k, (l, r) in enumerate(prods):
                        last = nc.tensor.matmul(ps_g, l, r, start=k == 0, stop=k == 5)
                elif name[:4] == "pair":
                    p = int(name[4])
                    pe.wait_ge(w.ctx_lo_made, nb + 1)
                    cols = slice(p * P, p * P + P)
                    for i, (wt, hi, lo) in enumerate(((wq1, w.xT_hi, w.xT_lo), (wk1, w.ctxT_hi, w.ctxT_lo))):
                        prods = [x for c in range(2) for x in terms(wt[:, 0, c, cols], wt[:, 1, c, cols],
                                                                    hi[:, c, :], lo[:, c, :])]
                        for k, (l, r) in enumerate(prods):
                            last = nc.tensor.matmul(halves(ps_g)[:, i, :], l, r, start=k == 0, stop=k == 5)
                elif name == "xT":
                    pe.wait_ge(w.xn_made, nb + 1)
                    last = pe_transposes(w.xn, ps_g)
                elif name == "shift":
                    pe.wait_ge(x3n_made, nb + 1)
                    last = pe_transposes(x3n, ps_g)
                elif name == "mix_k":
                    pe.wait_ge(mix_lo_made, nb + 1)
                    for m in range(DT):
                        mm = slice(m * P, m * P + P)
                        prods = [x for c in range(DT) for x in terms(wf[:, 0, 1, c, mm], wf[:, 1, 1, c, mm],
                                                                     mix_hi[:, 1, c, :], mix_lo[:, 1, c, :])]
                        for k, (l, r) in enumerate(prods):
                            last = nc.tensor.matmul(halves(ps_g)[:, m, :], l, r, start=k == 0, stop=k == 5)
                else:
                    if name == "mix_v":
                        pe.wait_ge(ka_lo_made, nb + 1)
                    i, hi, lo = (0, mix_hi[:, 0], mix_lo[:, 0]) if name == "mix_r" else (2, ka_hi, ka_lo)
                    for t in range(NT):
                        tt = slice(t * P, t * P + P)
                        prods = [x for c in range(DT) for x in terms(hi[:, c, tt], lo[:, c, tt],
                                                                     wf[:, 0, i, c, :], wf[:, 1, i, c, :])]
                        for k, (l, r) in enumerate(prods):
                            last = nc.tensor.matmul(halves(ps_g)[:, t, :], l, r, start=k == 0, stop=k == 5)
                last.then_inc(w.g_ready, 1)

            def scores(b, has, n):
                p, r = n // 2, slice(HD1 * (n % 2), HD1 * (n % 2) + HD1)
                if n % 2 == 0:
                    if p < 2:
                        pe.wait_ge(w.g_lo, base_of(USES3, b)[2] - 1)
                    else:
                        pe.wait_ge(w.g_lo, use_of(USES3, b, has, (2 * p - 4, 1))[4] + 1)
                pe.wait_ge(w.exp_ready, since(unit3(b, n) - 1))
                bank = halves(ps_s[:, n % 2, :])
                for q in range(NT):
                    qq = slice(q * P, q * P + P)
                    for k, (l, rr) in enumerate(terms(qk_hi[r, p % 2, 0, qq], qk_lo[r, p % 2, 0, qq],
                                                      qk_hi[r, p % 2, 1, :], qk_lo[r, p % 2, 1, :])):
                        last = nc.tensor.matmul(bank[:, q, :], l, rr, start=k == 0, stop=k == 2)
                last.then_inc(w.scores_ready, 1)

            def product(b, has, n):
                h, nb = (n, b) if n >= 0 else (n + H, b - 1)
                p = h // 2
                pe.wait_ge(w.prob_lo_ready, unit3(b, n) + 1)
                if h % 2 == 0:
                    pe.wait_ge(w.oT_lo_ready, since(nb * HP + p - 1))
                if h == 0:
                    pe.wait_ge(w.g_lo, base_of(USES3, b)[2])
                if h == H // 2:
                    pe.wait_ge(w.g_lo, use_of(USES3, b, has, (9, 1))[4] + 1)
                cols = slice(p * P, p * P + P)
                prods = [x for k in range(NT) for x in terms(v1_hi[:, k, cols], v1_lo[:, k, cols],
                                                             w.prob_hi[:, n % 2, k, :], w.prob_lo[:, n % 2, k, :])]
                for k, (l, r) in enumerate(prods):
                    last = nc.tensor.matmul(halves(ps_o[:, p % 2, :])[:, h % 2, :], l, r, start=k == 0, stop=k == 5)
                last.then_inc(w.pv_done, 1)

            def turn(b, has):
                for n in range(H):
                    if unit3(b, n) is not None:
                        scores(b, has, n)
                    use_g(b, has, (n, 0))
                    if unit3(b, n - 2) is not None:
                        pe_unit_transposes(pe, w, unit3(b, n - 2), (n - 2) % 4)
                    if n % 2 == 1:
                        p, off = pair_of(n - 1)
                        if has_pair(b, off):
                            pe_out_proj(pe, w, b + off, p, HP, wo1)
                    if unit3(b, n - 4) is not None:
                        product(b, has, n - 4)
                    use_g(b, has, (n, 1))

            turns(pe, turn)

        def part3_act(act):
            w = u3
            for i, (wt, place_, kp, _, _, scale) in enumerate(W3):
                n = wt.shape[2]
                act.wait_ge(raw_loaded[i % 2], 16 * (i // 2 + 1))
                nc.scalar.activation(wt[:, 0, :], place_[0:kp, 0:n], ACT.Copy, scale=scale).then_inc(w3_hi, 1)

            def copy_g(b, has, key):
                use = use_of(USES3, b, has, key)
                if use is None or not USES3[key][2]:
                    return
                name, off, number, _, _ = use
                nb = b + off
                act.wait_ge(w.g_ready, number + 1)
                if name[0] == "v":
                    t, half = int(name[1]) % 2, int(name[1]) // 2
                    act.wait_ge(w.pv_done, since(nb * H - (H // 2 if half == 0 else 0)))
                    nc.scalar.activation(v1_hi[:, t, half * 512:half * 512 + 512], ps_g, ACT.Copy).then_inc(w.g_hi, 1)
                elif name[:4] == "pair":
                    p = int(name[4])
                    act.wait_ge(w.scores_ready, since(nb * H + 2 * p - 2))
                    nc.scalar.activation(qk_hi[:, p % 2, :, :], halves(ps_g), ACT.Copy).then_inc(w.g_hi, 1)
                elif name == "xT":
                    nc.scalar.activation(w.xT_hi[:, :, :], halves(ps_g), ACT.Copy).then_inc(w.g_hi, 1)
                elif name == "shift":
                    act.wait_ge(mix_made, nb)
                    nc.scalar.activation(xs[:, :, 1:N + 1], halves(ps_g), ACT.Copy).then_inc(w.g_hi, 1)
                else:
                    act.wait_ge(ka_lo_made, nb)
                    nc.scalar.activation(scratch[:, 0, :, :], halves(ps_g), ACT.Relu).then_inc(w.g_hi, 1)

            def turn(b, has):
                for n in range(H):
                    if unit3(b, n - 3) is not None:
                        act_unit_hi(act, w, unit3(b, n - 3), (n - 3) % 4)
                    if n % 2 == 0:
                        p, off = pair_of(n)
                        if has_pair(b, off):
                            act.wait_ge(w.pv_done, (b + off) * H + 2 * p + 2)
                            act.wait_ge(w.oproj_done, since((b + off) * HP + p - 1))
                            for i in range(2):
                                r = slice(HD1 * i, HD1 * i + HD1)
                                last = nc.scalar.activation(w.oT_hi[r, p % 2, :], halves(ps_o[:, p % 2, :])[r, i, :],
                                                            ACT.Copy)
                            last.then_inc(w.oT_hi_ready, 1)
                    copy_g(b, has, (n - 1, 1))
                    if unit3(b, n) is not None:
                        act_unit_exp(act, w, unit3(b, n), n % 4)
                    if n in SPLIT_STEPS and 1 in has:
                        c = SPLIT_STEPS.index(n)
                        ee, to = slice(2 * c, 2 * c + 2), slice(2 * (c % 2), 2 * (c % 2) + 2)
                        act.wait_ge(comb_loaded, b * 16 + 32)
                        if c < 2:
                            act.wait_ge(w.g_ready, base_of(USES3, b)[0])
                        else:
                            act.wait_ge(w.g_ready, use_of(USES3, b, has, (1, 1))[2] + 1)
                        nc.scalar.activation(comb_s[:, 0, to, :], comb_raw[:, ee, :], ACT.Copy).then_inc(cs_hi, 1)
                        act.wait_ge(eo_loaded, b * 16 + 32)
                        nc.scalar.activation(eo_s[:, 0, to, :], eo_raw[:, ee, :], ACT.Copy).then_inc(cs_hi, 1)
                    if n == 9 and -1 in has:
                        act.wait_ge(mix_made, b)
                        act.wait_ge(w.g_ready, base_of(USES3, b)[0])
                        nc.scalar.activation(mix_hi[:, :, :, :], mixed[:, :, :, :], ACT.Copy).then_inc(mix_hi_made, 1)
                    if n == 11 and 1 in has:
                        act.wait_ge(w.ctx_loaded, b * 16 + 32)
                        if 0 in has:
                            act.wait_ge(w.g_ready, use_of(USES3, b, has, (10, 1))[2] + 1)
                        nc.scalar.activation(w.ctxT_hi[:, :, :], w.ctxT[:, :, :], ACT.Copy).then_inc(w.ctx_hi_made, 1)
                    if n == 13 and -1 in has:
                        act.wait_ge(ksq_done, b)
                        nc.scalar.activation(ka_hi[:, :, :], scratch[:, 1, :, :], ACT.Copy).then_inc(ka_hi_made, 1)
                        act.wait_ge(w.g_lo, use_of(USES3, b, has, (12, 0))[4] + 1)
                        nc.scalar.activation(gate[:, :, :], gate[:, :, :], ACT.Exp).then_inc(gate_exp, 1)
                    copy_g(b, has, (n, 0))
                if -1 in has:
                    act.wait_ge(out_made, b)
                    act.dma_start(out[b - 1, :, :].rearrange("(t p) d -> p t d", p=P), y_out[:, :, :]).then_inc(out_stored, 16)

            turns(act, turn)
            act.wait_ge(out_stored, 16 * B)

        def part3_dve(dve):
            w = u3
            for i, (wt, place_, kp, _, _, scale) in enumerate(W3):
                n = wt.shape[2]
                dve.wait_ge(w3_hi, i + 1)
                nc.vector.scalar_tensor_tensor(wt[:, 1, :], place_[0:kp, 0:n], scale, wt[:, 0, :].bitcast(F32),
                                               ALU.mult, ALU.subtract).then_inc(w3_lo, 1)
            dve.wait_ge(tables_loaded, 32)
            nc.vector.memset(xs[:, :, 0:1], 0.0).then_inc(tables_made, 1)
            for i in range(2):
                nc.vector.tensor_scalar(mu[:, i, 1, :], mu[:, i, 0, :], -1.0, 1.0, ALU.mult, ALU.add).then_inc(tables_made, 1)

            def read_g(b, has, key):
                use = use_of(USES3, b, has, key)
                if use is None or not USES3[key][3]:
                    return
                name, off, number, by_act, _ = use
                nb = b + off
                if USES3[key][2]:
                    dve.wait_ge(w.g_hi, by_act + 1)
                else:
                    dve.wait_ge(w.g_ready, number + 1)
                if name == "experts0":
                    dve.wait_ge(w.x_loaded, nb * 16 + 16)
                    dve.wait_ge(x2_made, nb)
                    nc.vector.tensor_tensor(x2_half[:, :, :], halves(ps_g), w.x_in[:, :, :], ALU.add).then_inc(w.g_lo, 1)
                elif name == "experts1":
                    dve.wait_ge(x2_biased, nb)
                    dve.wait_ge(w.g_lo, use_of(USES3, b, has, (1, 1))[4] + 1)
                    nc.vector.tensor_tensor(x2[:, :, :], halves(ps_g), x2_half[:, :, :], ALU.add).then_inc(w.g_lo, 1)
                elif name[0] == "v":
                    t, half = int(name[1]) % 2, int(name[1]) // 2
                    m = slice(half * 512, half * 512 + 512)
                    dve_lo(v1_lo[:, t, m], ps_g, v1_hi[:, t, m]).then_inc(w.g_lo, 1)
                elif name[:4] == "pair":
                    p = int(name[4])
                    dve_lo(qk_lo[:, p % 2, :, :], halves(ps_g), qk_hi[:, p % 2, :, :]).then_inc(w.g_lo, 1)
                elif name == "xT":
                    dve_lo(w.xT_lo[:, :, :], halves(ps_g), w.xT_hi[:, :, :]).then_inc(w.g_lo, 1)
                elif name == "mix_r":
                    dve.wait_ge(out_made, nb)
                    nc.vector.tensor_scalar(gate[:, :, :], halves(ps_g), -1.0, EXP_MAX, ALU.mult, ALU.min).then_inc(w.g_lo, 1)
                else:
                    dve.wait_ge(gate_step, nb * 2 + 2)
                    nc.vector.tensor_tensor(gate[:, :, :], halves(ps_g), gate[:, :, :], ALU.mult).then_inc(w.g_lo, 1)

            def turn(b, has):
                for n in range(H):
                    if unit3(b, n) is not None:
                        dve_unit_max(dve, w, unit3(b, n), n % 4)
                    if unit3(b, n - 1) is not None:
                        dve_unit_inv(dve, w, unit3(b, n - 1), (n - 1) % 4)
                    if unit3(b, n - 3) is not None:
                        dve_unit_lo(dve, w, unit3(b, n - 3), (n - 3) % 4)
                    if n % 2 == 0:
                        p, off = pair_of(n)
                        if has_pair(b, off):
                            dve.wait_ge(w.oT_hi_ready, (b + off) * HP + p + 1)
                            for i in range(2):
                                r = slice(HD1 * i, HD1 * i + HD1)
                                last = dve_lo(w.oT_lo[r, p % 2, :], halves(ps_o[:, p % 2, :])[r, i, :],
                                              w.oT_hi[r, p % 2, :])
                            last.then_inc(w.oT_lo_ready, 1)
                    read_g(b, has, (n - 1, 1))
                    if n in SPLIT_STEPS and 1 in has:
                        c = SPLIT_STEPS.index(n)
                        ee, to = slice(2 * c, 2 * c + 2), slice(2 * (c % 2), 2 * (c % 2) + 2)
                        dve.wait_ge(cs_hi, (b + 1) * 2 * PAIRS + 2 * c + 1)
                        dve_lo(comb_s[:, 1, to, :], comb_raw[:, ee, :], comb_s[:, 0, to, :]).then_inc(cs_lo, 1)
                    if n == 5 and -1 in has:
                        dve.wait_ge(w.oproj_done, b * HP)
                        dve.wait_ge(out_made, b - 1)
                        nc.vector.tensor_tensor(x3[:, :, :], halves(ps_y), x2_res[:, :, :], ALU.add).then_inc(w.sum_taken, 1)
                        dve.wait_ge(w.sum_taken, b)
                        dve_ln(dve, x3_norm, x3, (b - 1) * LN_STEPS, 0)
                    if n == 5 and 0 in has:
                        dve.wait_ge(x2_biased, b + 1)
                        nc.vector.tensor_copy(x2_res[:, :, :], x2_bias[:, :, :]).then_inc(x2_moved, 1)
                    if n == 6 and -1 in has:
                        dve_ln(dve, x3_norm, x3, (b - 1) * LN_STEPS, 1)
                        dve.wait_ge(w.g_ready, base_of(USES3, b)[0])
                        dve_normed(x3_norm, x3, x3n).then_inc(x3n_made, 1)
                    if n == 6 and 1 in has:
                        dve.wait_ge(w.g_lo, use_of(USES3, b, has, (5, 1))[4] + 1)
                        dve.sem_inc(x2_made, 1)
                    if n == 7 and 1 in has:
                        dve_ln(dve, x2_norm, x2, (b + 1) * LN_STEPS, 0)
                    if n == 8 and 1 in has:
                        dve_ln(dve, x2_norm, x2, (b + 1) * LN_STEPS, 1)
                        dve.wait_ge(w.g_ready, base_of(USES3, b)[0])
                        dve_normed(x2_norm, x2, w.xn).then_inc(w.xn_made, 1)
                    if n == 9 and -1 in has:
                        dve.wait_ge(w.g_hi, use_of(USES3, b, has, (7, 1))[3] + 1)
                        dve.wait_ge(ka_lo_made, b - 1)
                        for i in (1, 0):
                            for c in range(DT):
                                last = nc.vector.tensor_scalar(scratch[:, i, c, :], xs[:, c, 0:N], mu[:, i, 1, c:c + 1],
                                                               None, ALU.mult)
                        last.then_inc(mix_part_made, 1)
                        dve.wait_ge(mix_part_made, b)
                        dve.wait_ge(mix_lo_made, b - 1)
                        for i in (1, 0):
                            for c in range(DT):
                                last = nc.vector.scalar_tensor_tensor(mixed[:, i, c, :], xs[:, c, 1:N + 1],
                                                                      mu[:, i, 0, c:c + 1], scratch[:, i, c, :],
                                                                      ALU.mult, ALU.add)
                        last.then_inc(mix_made, 1)
                    if n == 12 and -1 in has:
                        dve.wait_ge(w.g_hi, use_of(USES3, b, has, (11, 1))[3] + 1)
                        nc.vector.tensor_tensor(scratch[:, 1, :, :], scratch[:, 0, :, :], scratch[:, 0, :, :],
                                                ALU.mult).then_inc(ksq_done, 1)
                    if n == 13 and -1 in has:
                        dve.wait_ge(gate_exp, b)
                        nc.vector.tensor_scalar(gate[:, :, :], gate[:, :, :], 1.0, None, ALU.add).then_inc(gate_step, 1)
                        dve.wait_ge(gate_step, b * 2 - 1)
                        nc.vector.reciprocal(gate[:, :, :], gate[:, :, :]).then_inc(gate_step, 1)
                    read_g(b, has, (n, 0))
                    if n == 15 and -1 in has:
                        dve.wait_ge(w.g_lo, use_of(USES3, b, has, (14, 0))[4] + 1)
                        dve.wait_ge(out_stored, b * 16 - 16)
                        nc.vector.tensor_tensor(y_out[:, :, :], gate[:, :, :], x3[:, :, :], ALU.add).then_inc(out_made, 1)

            turns(dve, turn)

        def part3_pool(pool):
            w = u3
            pool.wait_ge(tables_loaded, 32)

            def turn(b, has):
                for n in range(H):
                    if unit3(b, n - 1) is not None:
                        pool_unit_norm(pool, w, unit3(b, n - 1), (n - 1) % 4)
                    if n in SPLIT_STEPS and 1 in has:
                        c = SPLIT_STEPS.index(n)
                        ee, to = slice(2 * c, 2 * c + 2), slice(2 * (c % 2), 2 * (c % 2) + 2)
                        pool.wait_ge(cs_hi, (b + 1) * 2 * PAIRS + 2 * c + 2)
                        nc.gpsimd.tensor_tensor(eo_s[:, 1, to, :], eo_raw[:, ee, :], eo_s[:, 0, to, :].bitcast(F32),
                                                ALU.subtract).then_inc(es_lo, 1)
                    if n == 1 and 0 in has:
                        pool.wait_ge(x2_made, b + 1)
                        pool.wait_ge(x2_moved, b)
                        nc.gpsimd.tensor_tensor(x2_bias[:, :, :], x2[:, :, :],
                                                b_out[:, :].unsqueeze(1).to_broadcast([P, NT, D]),
                                                ALU.add).then_inc(x2_biased, 1)
                    if n == 9 and -1 in has:
                        pool.wait_ge(mix_hi_made, b)
                        nc.gpsimd.tensor_tensor(mix_lo[:, :, :, :].rearrange("p i c n -> p (i c n)"),
                                                mixed[:, :, :, :].rearrange("p i c n -> p (i c n)"),
                                                mix_hi[:, :, :, :].rearrange("p i c n -> p (i c n)").bitcast(F32),
                                                ALU.subtract).then_inc(mix_lo_made, 1)
                    if n == 11 and 1 in has:
                        pool.wait_ge(w.ctx_hi_made, b + 2)
                        nc.gpsimd.tensor_tensor(w.ctxT_lo[:, :, :], w.ctxT[:, :, :], w.ctxT_hi[:, :, :].bitcast(F32),
                                                ALU.subtract).then_inc(w.ctx_lo_made, 1)
                    if n == 13 and -1 in has:
                        pool.wait_ge(ka_hi_made, b)
                        nc.gpsimd.tensor_tensor(ka_lo[:, :, :], scratch[:, 1, :, :], ka_hi[:, :, :].bitcast(F32),
                                                ALU.subtract).then_inc(ka_lo_made, 1)

            turns(pool, turn)

        def part3_sp(sp):
            w = u3
            for i, (_, place_, kp, chunks, src, _) in enumerate(W3):
                n = W3[i][0].shape[2]
                if i > 1:
                    sp.wait_ge(w3_lo, i - 1)
                sp.dma_start(place_[0:kp, 0:n].rearrange("p (c n) -> p c n", c=chunks), src).then_inc(raw_loaded[i % 2], 16)
            sp.dma_start(mu[:, :, 0, :], a["mu"]).then_inc(tables_loaded, 16)
            sp.dma_start(b_out[:, :], a["b_out"].partition_broadcast(P)).then_inc(tables_loaded, 16)
            sp.wait_ge(w3_lo, len(W3))

            def turn(b, has):
                if 1 in has:
                    sp.wait_ge(x2_made, b + 1)
                    sp.sem_inc(sp_passed, 1)
                    sp.dma_start(w.x_in[:, :, :], x1_dram[b + 1, :, :, :]).then_inc(w.x_loaded, 16)
                    sp.wait_ge(cs_lo, (b + 1) * PAIRS)
                    sp.sem_inc(sp_passed, 1)
                    sp.dma_start(comb_raw[:, :, :], comb_dram[b + 1, :, :, :]).then_inc(comb_loaded, 16)
                    sp.wait_ge(es_lo, (b + 1) * PAIRS)
                    sp.sem_inc(sp_passed, 1)
                    sp.dma_start(eo_raw[:, :, :], eo_dram[:, :, b + 1, :].rearrange("e p d -> p e d")).then_inc(eo_loaded, 16)
                    sp.wait_ge(w.ctx_lo_made, b + 1)
                    sp.sem_inc(sp_passed, 1)
                    sp.dma_start(w.ctxT[:, :, :],
                                 a["ctxT"][b + 1, :, :].rearrange("(c p) n -> p c n", c=2)).then_inc(w.ctx_loaded, 16)

            turns(sp, turn)

        @block.tensor
        def _(pe):
            part1_pe(pe)
            end_part(pe, 0)
            part2_pe(pe)
            end_part(pe, 1)
            part3_pe(pe)

        @block.scalar
        def _(act):
            part1_act(act)
            end_part(act, 0)
            part2_act(act)
            end_part(act, 1)
            part3_act(act)

        @block.vector
        def _(dve):
            part1_dve(dve)
            end_part(dve, 0)
            part2_dve(dve)
            end_part(dve, 1)
            part3_dve(dve)

        @block.gpsimd
        def _(pool):
            part1_pool(pool)
            end_part(pool, 0)
            part2_pool(pool)
            end_part(pool, 1)
            part3_pool(pool)

        @block.sync
        def _(sp):
            part1_sp(sp)
            end_part(sp, 0)
            part2_sp(sp)
            end_part(sp, 1)
            part3_sp(sp)


def kernel(**inputs):
    import numpy as np
    import concourse.bacc as bacc
    from concourse.bass_utils import run_bass_kernel_spmd

    i = {k: np.asarray(v) for k, v in inputs.items()}
    heads, dim = 16, i["x"].shape[2]
    hd = dim // heads

    def twice(w):
        w = w.reshape(w.shape[0], heads, 1, hd)
        return np.concatenate([w, w], axis=2).reshape(w.shape[0], 2 * dim)

    wo = i["L0_xattn_Wo"].reshape(4, 4, 1, hd, dim)
    wo = np.concatenate([wo, wo], axis=2).reshape(4, P, dim).transpose(1, 0, 2)
    mu = np.stack([i["L1_ffn_mu_r"], i["L1_ffn_mu_k"]]).reshape(2, 2, P).transpose(2, 0, 1)
    b1 = i["L0_ffn_b1"]
    arrays = {
        "x": i["x"],
        "ctxT": i["ctx_768"].transpose(0, 2, 1),
        "mask": i["mask_BxS2_bf1"].view(np.uint8),
        "Wq0": twice(i["L0_xattn_Wq"]),
        "Wk0": twice(i["L0_xattn_Wk"]),
        "Wv0": i["L0_xattn_Wv"],
        "Wo0": wo,
        "gamma": i["L0_ffn_norm_gamma"],
        "gamma_s": i["L0_ffn_slot_norm_gamma"],
        "lo_rows": np.where(np.arange(P) % 32 >= 16, -1.0, 0.0).astype(np.float32).reshape(P, 1),
        "slots": i["L0_ffn_slot_embeds"],
        "w1": i["L0_ffn_w1"],
        "b1": b1.reshape(b1.shape[0], b1.shape[1] // P, P).transpose(0, 2, 1),
        "w2": i["L0_ffn_w2"],
        "b2": i["L0_ffn_b2"],
        "w_q": i["L1_xattn_w_q"],
        "w_k": i["L1_xattn_w_k"],
        "w_v": i["L1_xattn_w_v"],
        "w_out": i["L1_xattn_w_out"],
        "b_out": i["L1_xattn_b_out"],
        "wf": np.stack([i["L1_ffn_W_r"].T, i["L1_ffn_W_k"].T, i["L1_ffn_W_v"].T]),
        "mu": mu,
    }
    nc = bacc.Bacc("TRN2", target_bir_lowering=False, num_devices=1)
    fed, aps = {}, {}
    for name, v in arrays.items():
        v = np.ascontiguousarray(v)
        fed[f"in_{name}"] = v
        aps[name] = nc.dram_tensor(f"in_{name}", v.shape, mybir.dt.from_np(v.dtype), kind="ExternalInput").ap()
    out = nc.dram_tensor("out", i["x"].shape, F32, kind="ExternalOutput").ap()
    xattn_ffn_kernel(nc, aps, out)
    r = run_bass_kernel_spmd(nc, [fed], core_ids=[0])
    return r.results[0]["out"]
```

```python
from contextlib import ExitStack

import concourse.bass as bass
from concourse import mybir

F32 = mybir.dt.float32
F32R = mybir.dt.float32r
U8 = mybir.dt.uint8
I32 = mybir.dt.int32
ALU = mybir.AluOpType
ACT = mybir.ActivationFunctionType
AX = mybir.AxisListType

P = 128
MASKED = 2.0 ** 100
LN_EPS = 1e-5
EXP_MAX = 80.0
RMS_FLOOR = 1e-24
ROOT_GUESS = float(0x5F375A00)
LN_STEPS = 14
RMS_STEPS = 15



def terms(a_hi, a_lo, b_hi, b_lo):
    return ((a_hi, b_hi), (a_lo, b_hi), (a_hi, b_lo))


def halves(bank):
    return bank.rearrange("p (a n) -> p a n", a=2)


class Norm:

    def __init__(self, sb, sem, name, n):
        self.n = n
        self.bn = sb(f"{name}_bn", [P, n, 6], F32)
        self.mv = sb(f"{name}_mv", [P, n, 2], F32)
        self.v = sb(f"{name}_v", [P, 2, n], F32)
        self.half = sb(f"{name}_half", [P, n], I32)
        self.root = sb(f"{name}_root", [P, 3, n], F32)
        self.step = sem(f"{name}_step")


class Buffers:

    def __init__(self, sb, sem, i, KC, N, D):
        NT, DT = N // P, D // P
        self.x_in = sb(f"x_in{i}", [P, NT, D], F32)
        self.xn = sb(f"xn{i}", [P, NT, D], F32)
        self.xT_hi = sb(f"xT_hi{i}", [P, DT, N], F32R)
        self.xT_lo = sb(f"xT_lo{i}", [P, DT, N], F32R)
        self.ctxT = sb(f"ctxT{i}", [KC, 2, N], F32)
        self.ctxT_hi = sb(f"ctxT_hi{i}", [KC, 2, N], F32R)
        self.ctxT_lo = sb(f"ctxT_lo{i}", [KC, 2, N], F32R)
        self.ex = sb(f"ex{i}", [P, 4, 2, 256], F32)
        self.prob_hi = sb(f"prob_hi{i}", [P, 2, 2, 256], F32R)
        self.prob_lo = sb(f"prob_lo{i}", [P, 2, 2, 256], F32R)
        self.neg_max = sb(f"neg_max{i}", [P, 4, 2], F32)
        self.row_sum = sb(f"row_sum{i}", [P, 4, 2], F32)
        self.row_inv = sb(f"row_inv{i}", [P, 4, 2], F32)
        self.oT_hi = sb(f"oT_hi{i}", [P, 2, N], F32R)
        self.oT_lo = sb(f"oT_lo{i}", [P, 2, N], F32R)
        self.scores_ready = sem(f"scores_ready{i}")
        self.max_ready = sem(f"max_ready{i}")
        self.exp_ready = sem(f"exp_ready{i}")
        self.inv_ready = sem(f"inv_ready{i}")
        self.norm_ready = sem(f"norm_ready{i}")
        self.trans_ready = sem(f"trans_ready{i}")
        self.prob_hi_ready = sem(f"prob_hi_ready{i}")
        self.prob_lo_ready = sem(f"prob_lo_ready{i}")
        self.pv_done = sem(f"pv_done{i}")
        self.oT_hi_ready = sem(f"oT_hi_ready{i}")
        self.oT_lo_ready = sem(f"oT_lo_ready{i}")
        self.oproj_done = sem(f"oproj_done{i}")
        self.sum_taken = sem(f"sum_taken{i}")
        self.g_ready = sem(f"g_ready{i}")
        self.g_hi = sem(f"g_hi{i}")
        self.g_lo = sem(f"g_lo{i}")
        self.ctx_hi_made = sem(f"ctx_hi_made{i}")
        self.ctx_lo_made = sem(f"ctx_lo_made{i}")
        self.x_loaded = sem(f"x_loaded{i}")
        self.ctx_loaded = sem(f"ctx_loaded{i}")
        self.xn_made = sem(f"xn_made{i}")


def xattn_ffn_kernel(nc, a, out):
    B, N, D = a["x"].shape
    C = a["ctxT"].shape[1]
    KC = C // 2
    H = 16
    HD0 = D // H
    A1 = a["w_q"].shape[1]
    HD1 = A1 // H
    E, S, _ = a["slots"].shape
    HID = a["w1"].shape[2]
    NT = N // P
    DT = D // P
    G = 4
    GH = H // G
    RH = 2 * HD0
    MOVES = 4 * GH + 1
    VW = P + 32
    M = E * S
    PAIRS = E // 2
    HT = HID // P
    HP = H // 2
    BH = B // 2
    assert N == 256 and D == 256 and S == P and HD0 == 16 and HD1 == 64 and B == 8 and HT == 8

    x1_dram = nc.dram_tensor("x1_dram", (B, P, NT, D), F32, kind="Internal").ap()
    slots_dram = nc.dram_tensor("slots_dram", (E, P, DT, B, S), F32, kind="Internal").ap()
    comb_dram = nc.dram_tensor("comb_dram", (B, P, E, N), F32, kind="Internal").ap()
    eo_dram = nc.dram_tensor("eo_dram", (E, P, B, D), F32, kind="Internal").ap()

    with ExitStack() as ctx:
        place = ExitStack()

        def sb(name, shape, dt):
            return place.enter_context(nc.sbuf_tensor(name, shape, dt))

        def sem(name):
            return ctx.enter_context(nc.semaphore(name))

        ps_s = ctx.enter_context(nc.psum_tensor("ps_s", [P, 2, 512], F32))
        ps_t = ctx.enter_context(nc.psum_tensor("ps_t", [P, 2, 512], F32))
        ps_o = ctx.enter_context(nc.psum_tensor("ps_o", [P, 2, 512], F32))
        ps_yg = ctx.enter_context(nc.psum_tensor("ps_yg", [P, 2, 512], F32))
        ps_y = ps_yg[:, 0, :]
        ps_g = ps_yg[:, 1, :]

        ident = ctx.enter_context(nc.sbuf_tensor("ident", [P, P], F32))

        u1 = Buffers(sb, sem, "_1", KC, N, D)
        slot_norm = Norm(sb, sem, "slot_norm", E)
        x_norm = Norm(sb, sem, "x_norm", NT)
        r_norm = Norm(sb, sem, "r_norm", NT)
        x_res = sb("x_res", [P, NT, D], F32)
        wq0 = sb("wq0", [P, 2, DT, 2 * D], F32R)
        wk0 = sb("wk0", [KC, 2, 2, 2 * D], F32R)
        wv0 = sb("wv0", [KC, 2, 2, D], F32R)
        wo0 = sb("wo0", [P, 2, G, D], F32R)
        snT = sb("snT", [P, 2, DT, M], F32R)
        rT_hi = sb("rT_hi", [P, DT, N], F32R)
        rT_lo = sb("rT_lo", [P, DT, N], F32R)
        gamma = sb("gamma_sb", [P, D], F32)
        gamma_s = sb("gamma_s_sb", [P, D], F32)
        lo_rows = sb("lo_rows_sb", [P, 1], F32)
        mask_u8 = sb("mask_u8", [1, B * N], U8)
        mask_bias = sb("mask_bias", [1, B, N], F32R)
        q_rows = sb("q_rows", [2 * RH + 1, H, N], F32R)
        k_rows = sb("k_rows", [2 * RH + 1, H, N], F32R)
        q_full = sb("q_full", [P, 2, N], F32R)
        q_mix = sb("q_mix", [P, G, N], F32R)
        k_hi = sb("k_hi", [P, G, N], F32R)
        k_lo = sb("k_lo", [P, G, N], F32R)
        v_pad = sb("v_pad", [P, NT, G, GH * VW], F32R)
        x1 = sb("x1", [P, NT, D], F32)
        xc = sb("xc", [P, NT, D], F32)
        xr = sb("xr", [P, NT, D], F32)
        xr_hi = sb("xr_hi", [P, NT, D], F32R)
        xr_lo = sb("xr_lo", [P, NT, D], F32R)
        logit = sb("logit", [P, NT, M], F32)
        with ExitStack() as sub:
            raw0 = sub.enter_context(nc.sbuf_tensor("raw0", [P, 3584], F32))
            slot_raw = sub.enter_context(nc.sbuf_tensor("slot_raw", [P, E, D], F32))
        comb = sb("comb", [P, NT, M], F32)
        comb_stat = sb("comb_stat", [P, 3, NT], F32)
        combT = sb("combT", [P, E, N], F32)
        slot_out = sb("slot_out", [P, PAIRS, DT, N], F32)
        place.close()

        def both(name, shape, dt):
            return ctx.enter_context(nc.sbuf_tensor(name, shape, dt))

        wq1 = both("wq1", [P, 2, DT, A1], F32R)
        wk1 = both("wk1", [KC, 2, 2, A1], F32R)
        wv1 = both("wv1", [KC, 2, 2, A1], F32R)
        wo1 = both("wo1", [P, 2, HP, D], F32R)
        wf = both("wf_sb", [P, 2, 3, DT, D], F32R)
        comb_raw = both("comb_raw", [P, E, N], F32)
        eo_raw = both("eo_raw", [P, E, D], F32)

        w1_raw = sb("w1_raw", [P, DT, HID], F32)
        w2_raw = sb("w2_raw", [P, HT, D], F32)
        sl_raw = sb("sl_raw", [P, DT, B * S], F32)
        w1_s = sb("w1_s", [P, 2, DT, HID], F32R)
        w2_s = sb("w2_s", [P, 2, HT, D], F32R)
        sl_s = sb("sl_s", [P, 2, DT, B * S], F32R)
        b1_sb = sb("b1_sb", [P, E, HT], F32)
        b2_sb = sb("b2_sb", [P, E, D], F32)
        h_raw = sb("h_raw", [P, 2, 512], F32)
        h_hi = sb("h_hi", [P, 4, 512], F32R)
        h_lo = sb("h_lo", [P, 4, 512], F32R)
        eo = sb("eo", [P, 2, 2, 2, D], F32)
        place.close()

        u3 = Buffers(sb, sem, "_3", KC, N, D)
        x2_norm = Norm(sb, sem, "x2_norm", NT)
        x3_norm = Norm(sb, sem, "x3_norm", NT)
        qk_hi = sb("qk_hi", [P, 2, 2, N], F32R)
        qk_lo = sb("qk_lo", [P, 2, 2, N], F32R)
        x2_half = sb("x2_half", [P, NT, D], F32)
        x2 = sb("x2", [P, NT, D], F32)
        x2_bias = sb("x2_bias", [P, NT, D], F32)
        x2_res = sb("x2_res", [P, NT, D], F32)
        x3n = sb("x3n", [P, NT, D], F32)
        x3 = sb("x3", [P, NT, D], F32)
        b_out = sb("b_out_sb", [P, D], F32)
        mu = sb("mu_sb", [P, 2, 2, DT], F32)
        xs = sb("xs", [P, DT, N + 1], F32)
        gate = sb("gate", [P, NT, D], F32)
        scratch = sb("scratch", [P, 2, DT, N], F32)
        ka_hi = sb("ka_hi", [P, DT, N], F32R)
        ka_lo = sb("ka_lo", [P, DT, N], F32R)
        y_out = sb("y_out", [P, NT, D], F32)
        comb_s = sb("comb_s", [P, 2, E // 2, N], F32R)
        eo_s = sb("eo_s", [P, 2, E // 2, D], F32R)
        v1_hi = sb("v1_hi", [P, NT, A1], F32R)
        v1_lo = sb("v1_lo", [P, NT, A1], F32R)
        mixed = sb("mixed", [P, 2, DT, N], F32)
        mix_hi = sb("mix_hi", [P, 2, DT, N], F32R)
        mix_lo = sb("mix_lo", [P, 2, DT, N], F32R)
        place.close()

        dve_passed, sp_passed, act_passed = sem("dve_passed"), sem("sp_passed"), sem("act_passed")
        part_done = [sem(f"part_done{i}") for i in range(2)]
        wq0_loaded, wk0_loaded, wv0_loaded, wo0_loaded = (sem(f"{n}0_loaded") for n in ("wq", "wk", "wv", "wo"))
        slots_loaded = sem("slots_loaded")
        small_loaded = sem("small_loaded")
        early_loaded = sem("early_loaded")
        consts_made = sem("consts_made")
        w0_hi = sem("w0_hi")
        w0_lo = sem("w0_lo")
        slots_normed = sem("slots_normed")
        snT_ready = sem("snT_ready")
        snT_hi = sem("snT_hi")
        snT_lo = sem("snT_lo")
        res_loaded = sem("res_loaded")
        mask_made = sem("mask_made")
        qk_moved = [sem(f"qk_moved{i}") for i in range(2)]
        x1_stored = sem("x1_stored")
        xc_made = sem("xc_made")
        xr_made = sem("xr_made")
        xr_hi_made = sem("xr_hi_made")
        xr_lo_made = sem("xr_lo_made")
        cmax_ready = sem("cmax_ready")
        cexp_ready = sem("cexp_ready")
        cinv_ready = sem("cinv_ready")
        comb_ready = sem("comb_ready")
        comb_stored = sem("comb_stored")
        slot_copied = sem("slot_copied")
        slots_stored = sem("slots_stored")
        sl_loaded = sem("sl_loaded")
        first_loaded = [sem(f"first_loaded{i}") for i in range(3)]
        w1_loaded = sem("w1_loaded")
        w2_loaded = sem("w2_loaded")
        b_loaded = sem("b_loaded")
        e_hi = sem("e_hi")
        e_lo_dve = sem("e_lo_dve")
        e_lo_pool = sem("e_lo_pool")
        h_ready = sem("h_ready")
        gelu_done = sem("gelu_done")
        h_hi_made = sem("h_hi_made")
        h_lo_made = sem("h_lo_made")
        eo_part = sem("eo_part")
        eo_made = sem("eo_made")
        eo_stored = [sem(f"eo_stored{i}") for i in range(2)]
        raw_loaded = [sem("raw_loaded0"), sem("raw_loaded1")]
        w3_hi = sem("w3_hi")
        w3_lo = sem("w3_lo")
        tables_loaded = sem("tables_loaded")
        tables_made = sem("tables_made")
        comb_loaded = sem("comb_loaded")
        eo_loaded = sem("eo_loaded")
        cs_hi = sem("cs_hi")
        cs_lo = sem("cs_lo")
        es_lo = sem("es_lo")
        x2_made = sem("x2_made")
        x2_moved = sem("x2_moved")
        x3n_made = sem("x3n_made")
        mix_part_made = sem("mix_part_made")
        x2_biased = sem("x2_biased")
        mix_made = sem("mix_made")
        mix_hi_made = sem("mix_hi_made")
        mix_lo_made = sem("mix_lo_made")
        gate_exp = sem("gate_exp")
        gate_step = sem("gate_step")
        ksq_done = sem("ksq_done")
        ka_hi_made = sem("ka_hi_made")
        ka_lo_made = sem("ka_lo_made")
        out_made = sem("out_made")
        out_stored = sem("out_stored")

        block = ctx.enter_context(nc.Block())

        NU1 = H + PAIRS
        SPLIT_STEPS = (0, 1, 3, 4)
        HU = 2 * HT
        NSPLIT = 10

        def at(b, per, k):
            return b * per + max(k, 0)

        def end_part(engine, i):
            engine.drain().then_inc(part_done[i], 1)
            engine.wait_ge(part_done[i], 5)

        def pe_transposes(src, bank):
            for c in range(DT):
                for t in range(NT):
                    last = nc.tensor.transpose(halves(bank)[:, c, t * P:t * P + P], src[:, t, c * P:c * P + P],
                                               ident[:, :])
            return last

        def since(v):
            return max(v, 0) if isinstance(v, int) else v

        def pe_unit_transposes(pe, w, u, m):
            pe.wait_ge(w.norm_ready, since(u + 1))
            pe.wait_ge(w.prob_lo_ready, since(u - 1))
            bank = halves(ps_t[:, m % 2, :])
            for k in range(2):
                for q in range(2):
                    last = nc.tensor.transpose(bank[:, k, q * P:q * P + P], w.ex[:, m, q, k * P:k * P + P],
                                               ident[:, :])
            last.then_inc(w.trans_ready, 1)

        def pe_out_proj(pe, w, b, g, groups, wo):
            pe.wait_ge(w.oT_hi_ready, b * groups + g + 1)
            pe.wait_ge(w.oT_lo_ready, b * groups + g + 1)
            if g == 0:
                pe.wait_ge(w.sum_taken, b)
            for t in range(NT):
                tt = slice(t * P, t * P + P)
                for i, (l, r) in enumerate(terms(w.oT_hi[:, g % 2, tt], w.oT_lo[:, g % 2, tt],
                                                 wo[:, 0, g, :], wo[:, 1, g, :])):
                    last = nc.tensor.matmul(halves(ps_y)[:, t, :], l, r, start=g == 0 and t == 0 and i == 0,
                                            stop=g == groups - 1 and i == 2, skip_group_check=True)
            last.then_inc(w.oproj_done, 1)

        def act_unit_exp(act, w, u, m):
            act.wait_ge(w.max_ready, since(u + 1))
            act.wait_ge(w.trans_ready, since(u - 3))
            act.wait_ge(w.inv_ready, since(u - 3))
            for q in range(2):
                last = nc.scalar.activation(w.ex[:, m, q, :], halves(ps_s[:, m % 2, :])[:, q, :], ACT.Exp,
                                            bias=w.neg_max[:, m, q:q + 1], accum_out=w.row_sum[:, m, q:q + 1])
            last.then_inc(w.exp_ready, 1)

        def act_unit_hi(act, w, u, m):
            act.wait_ge(w.trans_ready, since(u + 1))
            act.wait_ge(w.pv_done, since(u - 1))
            nc.scalar.activation(w.prob_hi[:, m % 2, :, :], halves(ps_t[:, m % 2, :]),
                                 ACT.Copy).then_inc(w.prob_hi_ready, 1)

        def dve_unit_max(dve, w, u, m):
            dve.wait_ge(w.scores_ready, since(u + 1))
            dve.wait_ge(w.exp_ready, since(u - 3))
            nc.vector.tensor_reduce(w.neg_max[:, m, :], halves(ps_s[:, m % 2, :]), AX.X, ALU.max,
                                    negate=True).then_inc(w.max_ready, 1)

        def dve_unit_inv(dve, w, u, m):
            dve.wait_ge(w.exp_ready, since(u + 1))
            dve.wait_ge(w.norm_ready, since(u - 3))
            nc.vector.reciprocal(w.row_inv[:, m, :], w.row_sum[:, m, :]).then_inc(w.inv_ready, 1)

        def dve_lo(dst, full, hi):
            return nc.vector.tensor_tensor(dst, full, hi.bitcast(F32), ALU.subtract)

        def dve_unit_lo(dve, w, u, m):
            dve.wait_ge(w.prob_hi_ready, since(u + 1))
            dve.wait_ge(w.pv_done, since(u - 1))
            dve_lo(w.prob_lo[:, m % 2, :, :], halves(ps_t[:, m % 2, :]),
                   w.prob_hi[:, m % 2, :, :]).then_inc(w.prob_lo_ready, 1)

        def pool_unit_norm(pool, w, u, m):
            pool.wait_ge(w.inv_ready, since(u + 1))
            nc.gpsimd.tensor_tensor(w.ex[:, m, :, :], w.ex[:, m, :, :],
                                    w.row_inv[:, m, :].unsqueeze(2).to_broadcast([P, 2, 256]),
                                    ALU.mult).then_inc(w.norm_ready, 1)

        def dve_stats(dve, r, x, c):
            for t in range(r.n):
                last = nc.vector.bn_stats(r.bn[:, t, :], x[:, t, :])
            last.then_inc(r.step, 1)
            dve.wait_ge(r.step, c + 1)
            dve.sem_inc(dve_passed, 1)
            for t in range(r.n):
                last = nc.vector.bn_aggr(r.mv[:, t, :], r.bn[:, t, :])
            last.then_inc(r.step, 1)

        def dve_guess(dve, r, c):
            dve.wait_ge(r.step, c)
            nc.vector.tensor_scalar(r.half[:, :], r.v[:, 0, :].bitcast(I32), 1, None,
                                    ALU.logical_shift_right).then_inc(r.step, 1)
            dve.wait_ge(r.step, c + 1)
            nc.vector.tensor_scalar(r.root[:, 0, :].bitcast(I32), r.half[:, :], -1.0, ROOT_GUESS, ALU.mult,
                                    ALU.add).then_inc(r.step, 1)

        def dve_newton(dve, r, c):
            y, yy, vyy = r.root[:, 0, :], r.root[:, 1, :], r.root[:, 2, :]
            dve.wait_ge(r.step, c)
            nc.vector.tensor_tensor(yy, y, y, ALU.mult).then_inc(r.step, 1)
            dve.wait_ge(r.step, c + 1)
            nc.vector.scalar_tensor_tensor(vyy, yy, -0.5, r.v[:, 0, :], ALU.mult, ALU.mult).then_inc(r.step, 1)
            dve.wait_ge(r.step, c + 2)
            nc.vector.scalar_tensor_tensor(y, vyy, 1.5, y, ALU.add, ALU.mult).then_inc(r.step, 1)

        def dve_ln(dve, r, x, c, piece):
            if piece == 0:
                dve_stats(dve, r, x, c)
            elif piece == 1:
                dve.wait_ge(r.step, c + 2)
                nc.vector.tensor_scalar(r.v[:, 0, :], r.mv[:, :, 1], LN_EPS, None, ALU.add).then_inc(r.step, 1)
                dve_guess(dve, r, c + 3)
            else:
                dve_newton(dve, r, c + 5 + 3 * (piece - 2))
                if piece == 4:
                    dve.wait_ge(r.step, c + LN_STEPS)

        def dve_normed(r, x, dst):
            for t in range(NT):
                last = nc.vector.tensor_scalar(dst[:, t, :], x[:, t, :], r.mv[:, t, 0:1], r.root[:, 0, t:t + 1],
                                               ALU.subtract, ALU.mult)
            return last

        def turns(engine, turn, after_first=None):
            turn(-1, (1,))
            if after_first:
                after_first()
            turn(0, (0, 1))
            with engine.Fori(1, B - 1) as b:
                turn(b, (-1, 0, 1))
            turn(B - 1, (-1, 0))
            turn(B, (-1,))

        def base_of(uses, b):
            def count(i, off):
                return sum((1, u[2], u[3])[i] for u in uses.values() if u[1] == off)

            base = []
            for i in range(3):
                before, own, after = count(i, 1), count(i, 0), count(i, -1)
                if isinstance(b, int) and b <= 0:
                    base.append(before * (b + 1))
                elif isinstance(b, int) and b == B:
                    base.append(B * (before + own) + (B - 1) * after)
                else:
                    base.append(b * (before + own + after) + (before - after))
            return base

        def use_of(uses, b, has, key):
            if key not in uses or uses[key][1] not in has:
                return None
            before = [u for k, u in uses.items() if k < key and u[1] in has]
            number, by_act, by_dve = base_of(uses, b)
            return (uses[key][0], uses[key][1], number + len(before), by_act + sum(u[2] for u in before),
                    by_dve + sum(u[3] for u in before))

        RAW = {"wq0": slice(0, 1024), "wk0": slice(1024, 2048), "wv0": slice(2048, 2560), "wo0": slice(2560, 3584)}
        SEQ1 = [("head", h) for h in range(12)] + [("slots", j) for j in range(PAIRS)] + \
               [("head", h) for h in range(12, H)]
        USES1 = {0: ("q1", 0, 1, 1), 1: ("k1", 0, 1, 1), 3: ("v1", 0, 1, 1), 5: ("xT", 1, 1, 1), 7: ("q0", 1, 1, 1),
                 8: ("rT", -1, 1, 1), 9: ("logit0", -1, 1, 0), 10: ("logit1", -1, 1, 0), 11: ("logit2", -1, 1, 0),
                 12: ("logit3", -1, 1, 0), 13: ("k0", 1, 1, 1), 14: ("v0", 1, 1, 1), 16: ("comb0", -1, 1, 0),
                 17: ("comb1", -1, 1, 0), 18: ("comb2", -1, 1, 0), 19: ("comb3", -1, 1, 0)}

        def unit1(b, n):
            if isinstance(b, int) and b <= 0:
                if b < 0 or n < 0 or SEQ1[n][0] == "slots":
                    return None
                return SEQ1[n] + (SEQ1[n][1],)
            kind, k = SEQ1[n % NU1]
            if isinstance(b, int) and b == B and n >= 0:
                return (kind, k, B * NU1 - PAIRS + k) if kind == "slots" else None
            return kind, k, b * NU1 - PAIRS + n

        def use1(b, has, n):
            use = use_of(USES1, b, has, n)
            return use and (use[0], use[1], use[2], use[4])

        def part1_pe(pe):
            w = u1
            pe.wait_ge(w0_lo, 3)
            pe.wait_ge(consts_made, 4)

            def slot_transposes():
                pe.wait_ge(slots_normed, 2)
                for j in range(PAIRS):
                    if j > 1:
                        pe.wait_ge(snT_lo, j - 1)
                    bank = halves(ps_s[:, j % 2, :])
                    for c in range(DT):
                        for i in range(2):
                            last = nc.tensor.transpose(bank[:, c, i * P:i * P + P],
                                                       slot_raw[:, 2 * j + i, c * P:c * P + P], ident[:, :])
                    last.then_inc(snT_ready, 1)
                pe.wait_ge(snT_lo, PAIRS)
                pe.wait_ge(w0_lo, 4)

            def use_g(b, has, n):
                use = use1(b, has, n)
                if use is None:
                    return
                name, off, i, s = use
                pe.wait_ge(w.g_hi, since(i))
                pe.wait_ge(w.g_lo, since(s))
                kind, k = name[:-1], name[-1]
                if name == "xT":
                    pe.wait_ge(w.xn_made, b + off + 1)
                    last = pe_transposes(w.xn, ps_g)
                elif name == "rT":
                    pe.wait_ge(xr_made, b + off + 1)
                    last = pe_transposes(xr, ps_g)
                elif kind in ("q", "k"):
                    if kind == "k":
                        pe.wait_ge(w.ctx_lo_made, b + off + 1)
                    wt, src_hi, src_lo = (wq0, w.xT_hi, w.xT_lo) if kind == "q" else (wk0, w.ctxT_hi, w.ctxT_lo)
                    for i2 in range(2):
                        cols = slice((2 * int(k) + i2) * P, (2 * int(k) + i2 + 1) * P)
                        prods = [p for c in range(2) for p in terms(wt[:, 0, c, cols], wt[:, 1, c, cols],
                                                                    src_hi[:, c, :], src_lo[:, c, :])]
                        for m, (l, r) in enumerate(prods):
                            last = nc.tensor.matmul(halves(ps_g)[:, i2, :], l, r, start=m == 0, stop=m == 5)
                elif kind == "v":
                    cols = slice(int(k) * P, int(k) * P + P)
                    for t in range(NT):
                        tt = slice(t * P, t * P + P)
                        prods = [p for c in range(2) for p in terms(w.ctxT_hi[:, c, tt], w.ctxT_lo[:, c, tt],
                                                                    wv0[:, 0, c, cols], wv0[:, 1, c, cols])]
                        for m, (l, r) in enumerate(prods):
                            last = nc.tensor.matmul(ps_g[:, t * P:t * P + P], l, r, start=m == 0, stop=m == 5)
                elif kind == "logit":
                    t, half = int(k) % 2, int(k) // 2
                    tt, m = slice(t * P, t * P + P), slice(half * 512, half * 512 + 512)
                    prods = [p for c in range(DT) for p in terms(rT_hi[:, c, tt], rT_lo[:, c, tt],
                                                                 snT[:, 0, c, m], snT[:, 1, c, m])]
                    for m, (l, r) in enumerate(prods):
                        last = nc.tensor.matmul(ps_g, l, r, start=m == 0, stop=m == 5)
                else:
                    pe.wait_ge(comb_ready, (b + off) * NT + NT)
                    for i2 in range(2):
                        for t in range(NT):
                            m = (2 * int(k) + i2) * P
                            last = nc.tensor.transpose(halves(ps_g)[:, i2, t * P:t * P + P],
                                                       comb[:, t, m:m + P], ident[:, :])
                last.then_inc(w.g_ready, 1)

            def scores(b, has, n):
                kind, k, u = unit1(b, n)
                pe.wait_ge(w.exp_ready, since(u - 1))
                bank = halves(ps_s[:, n % 2, :])
                if kind == "head":
                    if k % (2 * GH) == 0:
                        pe.wait_ge(qk_moved[k // (2 * GH)], (b + 1) * MOVES * 16)
                    for q in range(NT):
                        last = nc.tensor.matmul(bank[:, q, :], q_rows[:, k, q * P:q * P + P], k_rows[:, k, :],
                                                start=True, stop=True)
                else:
                    pe.wait_ge(w.g_hi, use1(b, has, 10 if k < PAIRS // 2 else 12)[2] + 1)
                    for i in range(2):
                        for t in range(NT):
                            m = (2 * k + i) * P
                            last = nc.tensor.transpose(bank[:, i, t * P:t * P + P], logit[:, t, m:m + P], ident[:, :])
                last.then_inc(w.scores_ready, 1)

            def product(b, has, n):
                kind, k, u = unit1(b, n)
                hb = b - 1 if n < 0 else b
                m = n % 4
                pe.wait_ge(w.prob_lo_ready, since(u + 1))
                if kind == "head":
                    g = k // GH
                    if k % GH == 0:
                        if g in (0, 3):
                            pe.wait_ge(slot_copied, hb * PAIRS + g)
                        if g == 1:
                            pe.wait_ge(w.oT_lo_ready, hb * G)
                        elif g > 1:
                            pe.wait_ge(w.oT_lo_ready, hb * G + g - 1)
                    if k == 0:
                        pe.wait_ge(w.g_lo, base_of(USES1, b)[2])
                    if k == 2 * GH:
                        pe.wait_ge(w.g_lo, use1(b, has, 3)[3] + 1)
                    col = (k % GH) * P
                    for t in range(NT):
                        for i, pr in enumerate((w.prob_hi, w.prob_lo)):
                            last = nc.tensor.matmul(ps_o[:, g % 2, 0:N], v_pad[:, t, g, col:col + P], pr[:, m % 2, t, :],
                                                    start=k % GH == 0 and t == 0 and i == 0,
                                                    stop=k % GH == GH - 1 and t == NT - 1 and i == 1)
                else:
                    if k < 2 and 0 in has:
                        pe.wait_ge(w.oT_lo_ready, b * G + k + 2)
                    elif k < 2:
                        pe.wait_ge(w.oT_lo_ready, B * G)
                        pe.wait_ge(slot_copied, B * PAIRS)
                    else:
                        pe.wait_ge(slot_copied, b * PAIRS + k - 1)
                    pe.wait_ge(xr_hi_made, b)
                    pe.wait_ge(xr_lo_made, b)
                    for d in range(DT):
                        dd = slice(d * P, d * P + P)
                        prods = [p for t in range(NT) for p in terms(xr_hi[:, t, dd], xr_lo[:, t, dd],
                                                                     w.prob_hi[:, m % 2, t, :],
                                                                     w.prob_lo[:, m % 2, t, :])]
                        for i, (l, r) in enumerate(prods):
                            last = nc.tensor.matmul(halves(ps_o[:, (k + 1) % 2, :])[:, d, :], l, r,
                                                    start=i == 0, stop=i == 5)
                last.then_inc(w.pv_done, 1)

            def turn(b, has):
                for n in range(NU1):
                    if unit1(b, n):
                        scores(b, has, n)
                    if unit1(b, n - 2):
                        pe_unit_transposes(pe, w, unit1(b, n - 2)[2], (n - 2) % 4)
                    if n >= 16:
                        use_g(b, has, n)
                    if n in (9, 13, 17) and 0 in has:
                        pe_out_proj(pe, w, b, (n - 9) // 4, G, wo0)
                    if n == 5 and -1 in has:
                        pe_out_proj(pe, w, b - 1, 3, G, wo0)
                    if unit1(b, n - 4):
                        product(b, has, n - 4)
                    if n < 16:
                        use_g(b, has, n)

            turns(pe, turn, slot_transposes)

        def part1_act(act):
            w = u1
            def slot_hi():
                for j in range(PAIRS):
                    act.wait_ge(snT_ready, j + 1)
                    nc.scalar.activation(snT[:, 0, :, j * N:j * N + N], halves(ps_s[:, j % 2, :]),
                                         ACT.Copy).then_inc(snT_hi, 1)

            def copy_g(b, has, n):
                use = use1(b, has, n)
                if use is None:
                    return
                name, off, i, s = use
                act.wait_ge(w.g_ready, i + 1)
                kind, k = name[:-1], name[-1]
                if name == "xT":
                    nc.scalar.activation(w.xT_hi[:, :, :], halves(ps_g), ACT.Copy).then_inc(w.g_hi, 1)
                elif name == "rT":
                    nc.scalar.activation(rT_hi[:, :, :], halves(ps_g), ACT.Copy).then_inc(w.g_hi, 1)
                elif kind == "q":
                    act.wait_ge(w.g_lo, since(s))
                    nc.scalar.activation(q_full[:, :, :], halves(ps_g), ACT.Copy).then_inc(w.g_hi, 1)
                elif kind == "k":
                    j = int(k)
                    act.wait_ge(qk_moved[j], (b + off) * MOVES * 16)
                    nc.scalar.activation(k_hi[:, 2 * j:2 * j + 2, :], halves(ps_g), ACT.Copy).then_inc(w.g_hi, 1)
                elif kind == "v":
                    j = int(k)
                    act.wait_ge(consts_made, 4)
                    act.wait_ge(w.pv_done, since(units_of_half(b, j)))
                    vv = v_pad[:, :, 2 * j:2 * j + 2, :].rearrange("p t g (j w) -> p t (g j) w", w=VW)
                    for t in range(NT):
                        last = nc.scalar.activation(vv[:, t, :, 0:HD0],
                                                    ps_g[:, t * P:t * P + P].rearrange("p (j d) -> p j d", d=HD0),
                                                    ACT.Copy)
                    last.then_inc(w.g_hi, 1)
                elif kind == "logit":
                    t, half = int(k) % 2, int(k) // 2
                    act.wait_ge(cexp_ready, (b + off) * NT)
                    act.wait_ge(w.scores_ready, b * NU1 - PAIRS)
                    nc.scalar.activation(logit[:, t, half * 512:half * 512 + 512], ps_g, ACT.Copy).then_inc(w.g_hi, 1)
                else:
                    act.wait_ge(comb_stored, (b + off) * 16)
                    nc.scalar.activation(combT[:, 2 * int(k):2 * int(k) + 2, :], halves(ps_g),
                                         ACT.Copy).then_inc(w.g_hi, 1)

            def turn(b, has):
                if 1 in has:
                    act.wait_ge(w.xn_made, b + 1)
                    act.dma_start(w.x_in[:, :, :], a["x"][b + 1, :, :].rearrange("(t p) d -> p t d", p=P)).then_inc(w.x_loaded, 16)
                for n in range(NU1):
                    if n <= 16:
                        copy_g(b, has, n - 1)
                    if unit1(b, n - 3):
                        act_unit_hi(act, w, unit1(b, n - 3)[2], (n - 3) % 4)
                    if n in (8, 12, 16) and 0 in has:
                        copy_heads(b, n // 4 - 2)
                    if n == 4 and -1 in has:
                        copy_heads(b - 1, 3)
                    if unit1(b, n):
                        act_unit_exp(act, w, unit1(b, n)[2], n % 4)
                    if n == 5 and 1 in has:
                        act.wait_ge(w.ctx_loaded, b * 16 + 32)
                        if 0 in has:
                            act.wait_ge(w.g_ready, use1(b, has, 3)[2] + 1)
                        nc.scalar.activation(w.ctxT_hi[:, :, :], w.ctxT[:, :, :], ACT.Copy).then_inc(w.ctx_hi_made, 1)
                    if n == 9 and -1 in has:
                        act.wait_ge(xr_made, b)
                        act.wait_ge(w.pv_done, since(b * NU1 - 2 * PAIRS))
                        nc.scalar.activation(xr_hi[:, :, :], xr[:, :, :], ACT.Copy).then_inc(xr_hi_made, 1)
                    if n in (13, 14) and -1 in has:
                        t = n - 13
                        act.wait_ge(cmax_ready, (b - 1) * NT + t + 1)
                        act.wait_ge(cinv_ready, (b - 1) * NT)
                        act.wait_ge(w.g_ready, use1(b, has, 9)[2])
                        nc.scalar.activation(comb[:, t, :], logit[:, t, :], ACT.Exp, bias=comb_stat[:, 0, t:t + 1],
                                             accum_out=comb_stat[:, 1, t:t + 1]).then_inc(cexp_ready, 1)
                    if n >= 16:
                        copy_g(b, has, n)

            def copy_heads(b, g):
                act.wait_ge(w.pv_done, since(units_of_group(b, g)))
                act.wait_ge(w.oproj_done, since(b * G + g - 1))
                nc.scalar.activation(w.oT_hi[:, g % 2, :], ps_o[:, g % 2, 0:N], ACT.Copy).then_inc(w.oT_hi_ready, 1)

            turns(act, turn, slot_hi)

        def units_of_half(b, j):
            if j == 1 or (isinstance(b, int) and b < 0):
                return b * NU1 - PAIRS
            return b * NU1 + 2 * GH - (PAIRS if not isinstance(b, int) or b else 0)

        def units_of_group(b, g):
            if isinstance(b, int) and b == 0:
                return g * GH + GH
            return b * NU1 + g * GH + GH - (0 if g == G - 1 else PAIRS)

        def part1_dve(dve):
            w = u1
            def split(i, name, wt, kp, scale, loaded):
                full = raw0[0:kp, RAW[name]]
                hi = wt[:, 0, :, :].rearrange("p c n -> p (c n)")
                lo = wt[:, 1, :, :].rearrange("p c n -> p (c n)")
                dve.wait_ge(loaded, 16)
                nc.vector.tensor_scalar(hi, full, scale, None, ALU.mult).then_inc(w0_hi, 1)
                dve.wait_ge(w0_hi, i + 1)
                nc.vector.scalar_tensor_tensor(lo, full, scale, hi.bitcast(F32), ALU.mult,
                                               ALU.subtract).then_inc(w0_lo, 1)

            split(0, "wq0", wq0, P, HD0 ** -0.5, wq0_loaded)
            split(1, "wk0", wk0, KC, 1.0, wk0_loaded)
            split(2, "wv0", wv0, KC, 1.0, wv0_loaded)
            dve.wait_ge(early_loaded, 32)
            nc.vector.tensor_scalar(mask_bias[:, :, :].rearrange("p b n -> p (b n)"), mask_u8[:, :], -1.0,
                                    MASKED, ALU.add, ALU.mult).then_inc(mask_made, 1)

            def slot_norms():
                r = slot_norm
                dve.wait_ge(slots_loaded, 16)
                dve_stats(dve, r, slot_raw, 0)
                dve.wait_ge(r.step, 2)
                nc.vector.tensor_tensor(r.v[:, 1, :], r.mv[:, :, 0], r.mv[:, :, 0], ALU.mult).then_inc(r.step, 1)
                dve.wait_ge(r.step, 3)
                nc.vector.tensor_tensor(r.v[:, 1, :], r.v[:, 1, :], r.mv[:, :, 1], ALU.add).then_inc(r.step, 1)
                dve.wait_ge(r.step, 4)
                nc.vector.tensor_scalar(r.v[:, 0, :], r.v[:, 1, :], RMS_FLOOR / D, None, ALU.max).then_inc(r.step, 1)
                dve_guess(dve, r, 5)
                for k in range(3):
                    dve_newton(dve, r, 7 + 3 * k)
                dve.wait_ge(r.step, 16)
                for e in range(E):
                    last = nc.vector.tensor_scalar(slot_raw[:, e, :], slot_raw[:, e, :], r.root[:, 0, e:e + 1], None,
                                                   ALU.mult)
                last.then_inc(slots_normed, 1)
                dve.wait_ge(slots_normed, 1)
                dve.wait_ge(small_loaded, 32)
                nc.vector.tensor_tensor(slot_raw[:, :, :], slot_raw[:, :, :],
                                        gamma_s[:, :].unsqueeze(1).to_broadcast([P, E, D]), ALU.mult).then_inc(slots_normed, 1)
                split(3, "wo0", wo0, P, 1.0, wo0_loaded)
                for j in range(PAIRS):
                    dve.wait_ge(snT_hi, j + 1)
                    dve_lo(snT[:, 1, :, j * N:j * N + N], halves(ps_s[:, j % 2, :]),
                           snT[:, 0, :, j * N:j * N + N]).then_inc(snT_lo, 1)

            def copy_g(b, has, n):
                use = use1(b, has, n)
                if use is None or not USES1[n][3]:
                    return
                name, off, i, s = use
                dve.wait_ge(w.g_hi, i + 1)
                kind, k = name[:-1], name[-1]
                if name == "xT":
                    dve_lo(w.xT_lo[:, :, :], halves(ps_g), w.xT_hi[:, :, :]).then_inc(w.g_lo, 1)
                elif name == "rT":
                    dve_lo(rT_lo[:, :, :], halves(ps_g), rT_hi[:, :, :]).then_inc(w.g_lo, 1)
                elif kind == "q":
                    j = int(k)
                    dve.wait_ge(qk_moved[j], (b + off) * MOVES * 16)
                    qf = q_full[:, :, :].rearrange("p a n -> p (a n)").bitcast(F32)
                    nc.vector.scalar_tensor_tensor(q_mix[:, 2 * j:2 * j + 2, :].rearrange("p a n -> p (a n)"), qf,
                                                   lo_rows[:, 0:1], ps_g, ALU.mult, ALU.add).then_inc(w.g_lo, 1)
                elif kind == "k":
                    j = int(k)
                    dve_lo(k_lo[:, 2 * j:2 * j + 2, :], halves(ps_g), k_hi[:, 2 * j:2 * j + 2, :]).then_inc(w.g_lo, 1)
                else:
                    j = int(k)
                    vv = v_pad[:, :, 2 * j:2 * j + 2, :].rearrange("p t g (j w) -> p t (g j) w", w=VW)
                    for t in range(NT):
                        last = dve_lo(vv[:, t, :, HD0:2 * HD0],
                                      ps_g[:, t * P:t * P + P].rearrange("p (j d) -> p j d", d=HD0), vv[:, t, :, 0:HD0])
                    last.then_inc(w.g_lo, 1)

            def copy_heads(b, g):
                dve.wait_ge(w.oT_hi_ready, b * G + g + 1)
                dve_lo(w.oT_lo[:, g % 2, :], ps_o[:, g % 2, 0:N], w.oT_hi[:, g % 2, :]).then_inc(w.oT_lo_ready, 1)

            def copy_slots(b, j):
                dve.wait_ge(w.pv_done, b * NU1 + 2 * GH + j + 1 if not isinstance(b, int) or b < B else B * NU1 - PAIRS + j + 1)
                dve.wait_ge(slots_stored, (b - 1) * 16 * PAIRS * DT)
                nc.vector.tensor_copy(slot_out[:, j, :, :], halves(ps_o[:, (j + 1) % 2, :])).then_inc(slot_copied, 1)

            def turn(b, has):
                for n in range(NU1):
                    if unit1(b, n):
                        dve_unit_max(dve, w, unit1(b, n)[2], n % 4)
                    if unit1(b, n - 1):
                        dve_unit_inv(dve, w, unit1(b, n - 1)[2], (n - 1) % 4)
                    if n in (17, 18, 19) and -1 in has:
                        copy_slots(b, n - 17)
                    if n <= 15:
                        copy_g(b, has, n - 1)
                    if unit1(b, n - 3):
                        dve_unit_lo(dve, w, unit1(b, n - 3)[2], (n - 3) % 4)
                    if n in (8, 12, 16) and 0 in has:
                        copy_heads(b, n // 4 - 2)
                    if n == 4 and -1 in has:
                        copy_heads(b - 1, 3)
                    if n == 1 and 1 in has:
                        dve.wait_ge(w.x_loaded, b * 16 + 32)
                        dve_ln(dve, x_norm, w.x_in, (b + 1) * LN_STEPS, 0)
                    if n in (2, 3) and 1 in has:
                        dve_ln(dve, x_norm, w.x_in, (b + 1) * LN_STEPS, 2 * n - 3)
                        dve_ln(dve, x_norm, w.x_in, (b + 1) * LN_STEPS, 2 * n - 2)
                    if n == 4 and 1 in has:
                        if 0 in has:
                            dve.wait_ge(w.g_lo, use1(b, has, 0)[3])
                        dve_normed(x_norm, w.x_in, w.xn).then_inc(w.xn_made, 1)
                    if n == 5 and -1 in has:
                        dve.wait_ge(w.oproj_done, b * G)
                        dve.wait_ge(res_loaded, b * 16)
                        dve.wait_ge(x1_stored, b * 16 - 16)
                        nc.vector.tensor_tensor(x1[:, :, :], halves(ps_y), x_res[:, :, :], ALU.add).then_inc(w.sum_taken, 1)
                        dve.wait_ge(w.sum_taken, b)
                        dve_stats(dve, r_norm, x1, (b - 1) * RMS_STEPS)
                    if n == 6 and -1 in has:
                        r, c = r_norm, (b - 1) * RMS_STEPS
                        dve.wait_ge(r.step, c + 2)
                        nc.vector.tensor_scalar(r.v[:, 1, :], r.mv[:, :, 1], LN_EPS, RMS_FLOOR / D, ALU.add,
                                                ALU.mult).then_inc(r.step, 1)
                        dve.wait_ge(r.step, c + 3)
                        nc.vector.tensor_tensor(r.v[:, 0, :], r.v[:, 1, :], r.mv[:, :, 1], ALU.max).then_inc(r.step, 1)
                        dve_guess(dve, r, c + 4)
                        dve_newton(dve, r, c + 6)
                    if n == 7 and -1 in has:
                        r, c = r_norm, (b - 1) * RMS_STEPS
                        dve_newton(dve, r, c + 9)
                        dve_newton(dve, r, c + 12)
                        dve.wait_ge(r.step, c + 15)
                        dve.wait_ge(xr_made, b - 1)
                        dve_normed(r, x1, xc).then_inc(xc_made, 1)
                    if n in (12, 13) and -1 in has:
                        t = n - 12
                        dve.wait_ge(w.g_hi, use1(b, has, 11 + t)[2] + 1)
                        nc.vector.tensor_reduce(comb_stat[:, 0, t:t + 1], logit[:, t, :], AX.X, ALU.max,
                                                negate=True).then_inc(cmax_ready, 1)
                    if n == 15 and -1 in has:
                        for t in range(NT):
                            dve.wait_ge(cexp_ready, (b - 1) * NT + t + 1)
                            nc.vector.reciprocal(comb_stat[:, 2, t:t + 1], comb_stat[:, 1, t:t + 1]).then_inc(cinv_ready, 1)
                        for t in range(NT):
                            dve.wait_ge(cinv_ready, (b - 1) * NT + t + 1)
                            nc.vector.tensor_scalar(comb[:, t, :], comb[:, t, :], comb_stat[:, 2, t:t + 1], None,
                                                    ALU.mult).then_inc(comb_ready, 1)
                if isinstance(b, int) and b == 0:
                    dve.sem_inc(slot_copied, PAIRS)
                if -1 in has:
                    copy_slots(b, 3)

            turns(dve, turn, slot_norms)

        def part1_pool(pool):
            w = u1
            nc.gpsimd.memset(ident[:, :], 0.0).then_inc(consts_made, 1)
            pool.wait_ge(consts_made, 1)
            nc.gpsimd.affine_select(out=ident[:, :], in_=ident[:, :], compare_op=ALU.not_equal, fill=1.0, base=0,
                                    pattern=[[-1, P]], channel_multiplier=1).then_inc(consts_made, 1)
            pool.wait_ge(consts_made, 2)
            nc.gpsimd.memset(q_rows[2 * RH:2 * RH + 1, :, :].bitcast(F32), 1.0).then_inc(consts_made, 1)
            pool.wait_ge(consts_made, 3)
            nc.gpsimd.memset(v_pad[:, :, :, :].rearrange("p t g w -> p (t g w)").bitcast(F32),
                             0.0).then_inc(consts_made, 1)
            pool.wait_ge(small_loaded, 32)

            def turn(b, has):
                for n in range(NU1):
                    if unit1(b, n - 1):
                        pool_unit_norm(pool, w, unit1(b, n - 1)[2], (n - 1) % 4)
                    if n == 5 and 1 in has:
                        pool.wait_ge(w.ctx_hi_made, b + 2)
                        nc.gpsimd.tensor_tensor(w.ctxT_lo[:, :, :], w.ctxT[:, :, :], w.ctxT_hi[:, :, :].bitcast(F32),
                                                ALU.subtract).then_inc(w.ctx_lo_made, 1)
                    if n == 7 and -1 in has:
                        pool.wait_ge(xc_made, b)
                        pool.wait_ge(xr_lo_made, b - 1)
                        pool.wait_ge(w.g_ready, base_of(USES1, b)[0])
                        nc.gpsimd.tensor_tensor(xr[:, :, :], xc[:, :, :],
                                                gamma[:, :].unsqueeze(1).to_broadcast([P, NT, D]),
                                                ALU.mult).then_inc(xr_made, 1)
                    if n == 10 and -1 in has:
                        pool.wait_ge(xr_hi_made, b)
                        nc.gpsimd.tensor_tensor(xr_lo[:, :, :], xr[:, :, :], xr_hi[:, :, :].bitcast(F32),
                                                ALU.subtract).then_inc(xr_lo_made, 1)

            turns(pool, turn)

        def part1_sp(sp):
            w = u1
            for name, kp, src, loaded in (("wq0", P, a["Wq0"], wq0_loaded), ("wk0", KC, a["Wk0"], wk0_loaded),
                                          ("wv0", KC, a["Wv0"], wv0_loaded)):
                sp.dma_start(raw0[0:kp, RAW[name]].rearrange("p (c n) -> p c n", c=2),
                             src.rearrange("(c p) n -> p c n", c=2)).then_inc(loaded, 16)
            sp.dma_start(mask_u8[:, :], a["mask"].rearrange("b n -> (b n)").partition_broadcast(1)).then_inc(early_loaded, 16)
            sp.dma_start(lo_rows[:, :], a["lo_rows"]).then_inc(early_loaded, 16)
            sp.dma_start(raw0[:, RAW["wo0"]].rearrange("p (g n) -> p g n", g=G), a["Wo0"]).then_inc(wo0_loaded, 16)
            sp.dma_start(slot_raw[:, :, :], a["slots"].rearrange("e s d -> s e d")).then_inc(slots_loaded, 16)
            sp.dma_start(gamma_s[:, :], a["gamma_s"].partition_broadcast(P)).then_inc(small_loaded, 16)
            sp.dma_start(gamma[:, :], a["gamma"].partition_broadcast(P)).then_inc(small_loaded, 16)

            def move_half(b, batch, has, j):
                sp.wait_ge(w.g_lo, use1(b, has, 13 if j == 0 else 1)[3] + 1)
                sp.sem_inc(sp_passed, 1)
                sp.wait_ge(w.scores_ready, since(units_of_half(b, j)))
                sp.sem_inc(sp_passed, 1)
                gg = slice(2 * j, 2 * j + 2)
                for i in range(GH):
                    rows, hh = slice(RH * i, RH * i + RH), slice(2 * GH * j + i, 2 * GH * (j + 1), GH)
                    for dst, at_row, src in ((q_rows, 0, q_mix), (q_rows, RH, q_mix), (k_rows, 0, k_hi), (k_rows, RH, k_lo)):
                        sp.dma_start(dst[at_row:at_row + RH, hh, :].bitcast(F32), src[rows, gg, :].bitcast(F32)).then_inc(qk_moved[j], 16)
                sp.dma_start(k_rows[2 * RH:2 * RH + 1, 2 * GH * j:2 * GH * (j + 1), :].bitcast(F32),
                             mask_bias[0:1, batch, :].bitcast(F32).unsqueeze(1).to_broadcast([1, 2 * GH, N])).then_inc(qk_moved[j], 16)

            def turn(b, has):
                if isinstance(b, int) and b < 0:
                    sp.wait_ge(mask_made, 1)
                if 1 in has:
                    sp.wait_ge(w.ctx_lo_made, b + 1)
                    sp.sem_inc(sp_passed, 1)
                    sp.dma_start(w.ctxT[:, :, :],
                                 a["ctxT"][b + 1, :, :].rearrange("(c p) n -> p c n", c=2)).then_inc(w.ctx_loaded, 16)
                if 0 in has:
                    move_half(b, b, has, 1)
                if -1 in has:
                    sp.wait_ge(w.sum_taken, b)
                    sp.sem_inc(sp_passed, 1)
                    sp.dma_start(x1_dram[b - 1, :, :, :], x1[:, :, :]).then_inc(x1_stored, 16)
                if 0 in has:
                    sp.wait_ge(w.sum_taken, b)
                    sp.sem_inc(sp_passed, 1)
                    sp.dma_start(x_res[:, :, :], a["x"][b, :, :].rearrange("(t p) d -> p t d", p=P)).then_inc(res_loaded, 16)
                if 1 in has:
                    move_half(b, b + 1, has, 0)
                if -1 in has:
                    for j in range(PAIRS):
                        sp.wait_ge(slot_copied, b * PAIRS + j + 1)
                        sp.sem_inc(sp_passed, 1)
                        for d in range(DT):
                            sp.dma_start(slots_dram[2 * j:2 * j + 2, :, d, b - 1, :].rearrange("e p s -> p e s"),
                                         slot_out[:, j, d, :].rearrange("p (e s) -> p e s", e=2)).then_inc(slots_stored, 16)
                    sp.wait_ge(w.g_hi, use1(b, has, 19)[2] + 1)
                    sp.sem_inc(sp_passed, 1)
                    sp.dma_start(comb_dram[b - 1, :, :, :], combT[:, :, :]).then_inc(comb_stored, 16)

            turns(sp, turn)
            sp.wait_ge(x1_stored, 16 * B)
            sp.wait_ge(comb_stored, 16 * B)
            sp.wait_ge(slots_stored, 16 * B * PAIRS * DT)

        def split_pieces():
            def w1_piece(i):
                cols = slice(i * 2 * P, (i + 1) * 2 * P)
                return w1_raw[:, :, cols], w1_s[:, 0, :, cols], w1_s[:, 1, :, cols]

            def w2_piece(i):
                rows = slice(2 * i, 2 * i + 2)
                return w2_raw[:, rows, :], w2_s[:, 0, rows, :], w2_s[:, 1, rows, :]

            def sl_piece(i):
                cols = slice(i * 512, i * 512 + 512)
                return sl_raw[:, :, cols], sl_s[:, 0, :, cols], sl_s[:, 1, :, cols]

            pieces = [(sl_loaded, sl_piece(0))]
            for i in range(4):
                pieces += [(w1_loaded, w1_piece(i)), (w2_loaded, w2_piece(i))]
            return pieces + [(sl_loaded, sl_piece(1))]

        PIECES = split_pieces()
        h_banks = [ps_s[:, 0, :], ps_s[:, 1, :], ps_t[:, 0, :], ps_t[:, 1, :]]
        eo_banks = [ps_o, ps_yg]

        comb_flat = comb_raw[:, :, :].rearrange("p e n -> p (e n)")
        eo_flat = eo_raw[:, :, :].rearrange("p e n -> p (e n)")
        W3 = ((wq1[:, :, :, :].rearrange("p s c n -> p s (c n)"), comb_flat, P, 2,
               a["w_q"].rearrange("(c p) n -> p c n", c=2), HD1 ** -0.5),
              (wk1[:, :, :, :].rearrange("p s c n -> p s (c n)"), eo_flat, KC, 2,
               a["w_k"].rearrange("(c p) n -> p c n", c=2), 1.0),
              (wv1[:, :, :, :].rearrange("p s c n -> p s (c n)"), comb_flat, KC, 2,
               a["w_v"].rearrange("(c p) n -> p c n", c=2), 1.0),
              (wo1[:, :, :, :].rearrange("p s c n -> p s (c n)"), eo_flat, P, HP,
               a["w_out"].rearrange("(c p) n -> p c n", c=HP), 1.0),
              (wf[:, :, :, :, :].rearrange("p s i c n -> p s (i c n)"), comb_flat, P, 6,
               a["wf"].rearrange("i (c p) n -> p (i c) n", c=2), 1.0))
        W3_UNITS = tuple(range(3, 13))

        def weight_piece(k):
            wt, place_, kp, _, _, scale = W3[k // 2]
            n = wt.shape[2] // 2
            cols = slice((k % 2) * n, (k % 2) * n + n)
            return wt[:, 0, cols], wt[:, 1, cols], place_[0:kp, cols], scale

        def act_weight_hi(act, k):
            hi, _, raw, scale = weight_piece(k)
            act.wait_ge(raw_loaded[k // 2 % 2], 16 * (k // 4 + 1))
            nc.scalar.activation(hi, raw, ACT.Copy, scale=scale).then_inc(w3_hi, 1)

        def dve_weight_lo(dve, k):
            hi, lo, raw, scale = weight_piece(k)
            dve.wait_ge(w3_hi, k + 1)
            nc.vector.scalar_tensor_tensor(lo, raw, scale, hi.bitcast(F32), ALU.mult, ALU.subtract).then_inc(w3_lo, 1)

        def sp_weight(sp, i):
            wt, place_, kp, chunks, src, _ = W3[i]
            if i > 1:
                sp.wait_ge(w3_lo, 2 * i - 2)
            sp.dma_start(place_[0:kp, 0:wt.shape[2]].rearrange("p (c n) -> p c n", c=chunks), src).then_inc(raw_loaded[i % 2], 16)

        EARLY = {12: 0, 13: 1, 14: 2}

        def experts(engine, expert):
            expert(0, True, True)
            with engine.Fori(1, E - 1) as e:
                expert(e, True, True)
            expert(E - 1, True, False)
            expert(E, False, False)

        def part2_pe(pe):
            def hidden(e, n):
                half, hc = n // HT, n % HT
                if n == 0:
                    pe.wait_ge(e_lo_dve, e * 2 + 2)
                elif n < HT and n % 2 == 0:
                    pe.wait_ge(e_lo_pool, e * 8 + n)
                elif n == HT:
                    pe.wait_ge(e_lo_pool, e * 8 + 8)
                pe.wait_ge(gelu_done, since(e * HU + n - 3))
                cols, m = slice(hc * P, hc * P + P), slice(half * 512, half * 512 + 512)
                prods = [p for c in range(DT) for p in terms(w1_s[:, 0, c, cols], w1_s[:, 1, c, cols],
                                                             sl_s[:, 0, c, m], sl_s[:, 1, c, m])]
                for k, (l, r) in enumerate(prods):
                    last = nc.tensor.matmul(h_banks[n % 4], l, r, start=k == 0, stop=k == 5)
                last.then_inc(h_ready, 1)

            def output(e, u):
                half, hc = u // HT, u % HT
                pe.wait_ge(h_lo_made, e * HU + u + 1)
                if hc % 2 == 0 and half == 0:
                    pe.wait_ge(e_lo_pool, e * 8 + hc + 1)
                if hc == 0:
                    pe.wait_ge(eo_made, e * 4 + 2 * half - (2 if half else 2) if not isinstance(e, int) else max(e * 4 + 2 * half - 2, 0))
                for i in range(BH):
                    ss = slice(i * S, i * S + S)
                    for k, (l, r) in enumerate(terms(h_hi[:, u % 4, ss], h_lo[:, u % 4, ss],
                                                     w2_s[:, 0, hc, :], w2_s[:, 1, hc, :])):
                        last = nc.tensor.matmul(halves(eo_banks[half][:, i // 2, :])[:, i % 2, :], l, r,
                                                start=hc == 0 and i % 2 == 0 and k == 0,
                                                stop=hc == HT - 1 and k == 2, skip_group_check=True)
                last.then_inc(eo_part, 1)

            def expert(e, own, following):
                for n in range(HU if own else 2):
                    if own:
                        hidden(e, n)
                    if n >= 2:
                        output(e, n - 2)
                    elif not isinstance(e, int) or e > 0:
                        output(e - 1, n - 2 + HU)

            experts(pe, expert)

        def part2_act(act):
            def split_hi(e, i):
                loaded, (full, hi, _) = PIECES[i]
                if isinstance(e, int) and e == 0 and i < 3:
                    act.wait_ge(first_loaded[i], 16)
                else:
                    act.wait_ge(loaded, e * 16 + 16)
                if i == 0:
                    act.wait_ge(h_ready, since(e * HU - HT))
                elif i == 1:
                    act.wait_ge(h_ready, since(e * HU - HT + 2))
                elif i == 2:
                    act.wait_ge(eo_part, since(e * HU - HT + 2))
                else:
                    act.wait_ge(h_ready, e * HU)
                    act.wait_ge(eo_part, e * HU)
                nc.scalar.activation(hi, full, ACT.Copy).then_inc(e_hi, 1)

            for i in range(3):
                split_hi(0, i)
            act.wait_ge(b_loaded, 32)

            def expert(e, own, following):
                for n in range(HU if own else 0):
                    act.wait_ge(h_ready, e * HU + n + 1)
                    act.wait_ge(h_lo_made, since(e * HU + n - 1))
                    act.sem_inc(act_passed, 1)
                    nc.scalar.activation(h_raw[:, n % 2, :], h_banks[n % 4], ACT.Gelu,
                                         bias=b1_sb[:, e, n % HT:n % HT + 1]).then_inc(gelu_done, 1)
                    if n + 3 < NSPLIT:
                        split_hi(e, n + 3)
                    if n in EARLY and following:
                        split_hi(e + 1, EARLY[n])
                    if n in W3_UNITS and not following:
                        act_weight_hi(act, W3_UNITS.index(n))

            experts(act, expert)

        def part2_dve(dve):
            def split_lo(e, i):
                _, (full, hi, lo) = PIECES[i]
                dve.wait_ge(e_hi, e * NSPLIT + i + 1)
                dve_lo(lo, full, hi).then_inc(e_lo_dve, 1)

            for i in range(2):
                split_lo(0, i)
            dve.wait_ge(b_loaded, 32)

            def outputs(e, half):
                dve.wait_ge(eo_part, e * HU + HT * (half + 1))
                dve.wait_ge(eo_stored[half], e * 16)
                for i in range(2):
                    nc.vector.tensor_tensor(eo[:, half, i, :, :], halves(eo_banks[half][:, i, :]),
                                            b2_sb[:, e, :].unsqueeze(1).to_broadcast([P, 2, D]),
                                            ALU.add).then_inc(eo_made, 1)

            def expert(e, own, following):
                for n in range(HU if own else 3):
                    if own:
                        dve.wait_ge(gelu_done, e * HU + n + 1)
                        dve.wait_ge(eo_part, since(e * HU + n - 3))
                        nc.vector.tensor_copy(h_hi[:, n % 4, :], h_raw[:, n % 2, :]).then_inc(h_hi_made, 1)
                        dve.wait_ge(h_hi_made, e * HU + n + 1)
                        dve_lo(h_lo[:, n % 4, :], h_raw[:, n % 2, :], h_hi[:, n % 4, :]).then_inc(h_lo_made, 1)
                    if n == HT + 2:
                        outputs(e, 0)
                    if n == 2 and (not isinstance(e, int) or e > 0):
                        outputs(e - 1, 1)
                    if n in EARLY and EARLY[n] < 2 and following:
                        split_lo(e + 1, EARLY[n])
                    if n in W3_UNITS and own and not following:
                        dve_weight_lo(dve, W3_UNITS.index(n))

            experts(dve, expert)

        def part2_pool(pool):
            def split_lo(e, i):
                _, (full, hi, lo) = PIECES[i]
                pool.wait_ge(e_hi, e * NSPLIT + i + 1)
                nc.gpsimd.tensor_tensor(lo, full, hi.bitcast(F32), ALU.subtract).then_inc(e_lo_pool, 1)

            split_lo(0, 2)

            def expert(e, own, following):
                for i in range(3, NSPLIT if own else 0):
                    split_lo(e, i)
                if following:
                    split_lo(e + 1, 2)

            experts(pool, expert)

        def part2_sp(sp):
            def load(e):
                if not isinstance(e, int) or e > 0:
                    sp.wait_ge(e_lo_pool, e * 8)
                    sp.sem_inc(sp_passed, 1)
                    sp.wait_ge(e_lo_dve, e * 2)
                    sp.sem_inc(sp_passed, 1)
                sp.dma_start(sl_raw[:, :, :], slots_dram[e, :, :, :, :].rearrange("p t b s -> p t (b s)")).then_inc(sl_loaded, 16)
                sp.dma_start(w1_raw[:, :, :], a["w1"][e, :, :].rearrange("(c p) n -> p c n", p=P)).then_inc(w1_loaded, 16)
                sp.dma_start(w2_raw[:, :, :], a["w2"][e, :, :].rearrange("(h p) n -> p h n", p=P)).then_inc(w2_loaded, 16)

            def store(e, half):
                sp.wait_ge(eo_made, e * 4 + 2 * half + 2)
                sp.sem_inc(sp_passed, 1)
                sp.dma_start(eo_dram[e, :, half * BH:half * BH + BH, :],
                             eo[:, half, :, :, :].rearrange("p a i d -> p (a i) d")).then_inc(eo_stored[half], 16)

            sp.dma_start(sl_raw[:, :, 0:BH * S], slots_dram[0, :, :, 0:BH, :].rearrange("p t b s -> p t (b s)")).then_inc(first_loaded[0], 16)
            sp.dma_start(w1_raw[:, :, 0:2 * P], a["w1"][0, :, 0:2 * P].rearrange("(c p) n -> p c n", p=P)).then_inc(first_loaded[1], 16)
            sp.dma_start(w2_raw[:, 0:2, :], a["w2"][0, 0:2 * P, :].rearrange("(h p) n -> p h n", p=P)).then_inc(first_loaded[2], 16)
            sp.dma_start(w1_raw[:, :, 2 * P:HID], a["w1"][0, :, 2 * P:HID].rearrange("(c p) n -> p c n", p=P)).then_inc(w1_loaded, 16)
            sp.dma_start(w2_raw[:, 2:HT, :], a["w2"][0, 2 * P:HID, :].rearrange("(h p) n -> p h n", p=P)).then_inc(w2_loaded, 16)
            sp.dma_start(sl_raw[:, :, BH * S:B * S], slots_dram[0, :, :, BH:B, :].rearrange("p t b s -> p t (b s)")).then_inc(sl_loaded, 16)
            sp.dma_start(b1_sb[:, :, :], a["b1"].rearrange("e p h -> p e h")).then_inc(b_loaded, 16)
            sp.dma_start(b2_sb[:, :, :].rearrange("p e d -> p (e d)"),
                         a["b2"].rearrange("e d -> (e d)").partition_broadcast(P)).then_inc(b_loaded, 16)
            sp_weight(sp, 0)
            sp_weight(sp, 1)

            def expert(e, own, following):
                if not isinstance(e, int) or e > 0:
                    store(e - 1, 1)
                if following:
                    load(e + 1)
                if own and not following:
                    for i in range(2, len(W3)):
                        sp_weight(sp, i)
                if own:
                    store(e, 0)

            experts(sp, expert)
            sp.wait_ge(eo_stored[0], 16 * E)
            sp.wait_ge(eo_stored[1], 16 * E)

        USES3 = {(2 * p - 4, 1): (f"pair{p}", 0, 1, 1) for p in range(2, HP)} | {
            (2, 0): ("experts0", 1, 0, 1), (3, 1): ("v2", 0, 1, 1), (5, 1): ("experts1", 1, 0, 1),
            (7, 1): ("shift", -1, 1, 0), (9, 1): ("v3", 0, 1, 1), (11, 1): ("xT", 1, 1, 1),
            (12, 0): ("mix_k", -1, 1, 0), (12, 1): ("pair0", 1, 1, 1), (13, 0): ("mix_r", -1, 0, 1),
            (13, 1): ("v0", 1, 1, 1), (14, 0): ("v1", 1, 1, 1), (14, 1): ("pair1", 1, 1, 1),
            (15, 0): ("mix_v", -1, 0, 1)}

        def unit3(b, n):
            if isinstance(b, int) and ((b <= 0 and n < 0) or b < 0 or (b == B and n >= 0)):
                return None
            return b * H + n

        def pair_of(n):
            return ((n - 6) // 2, 0) if n >= 6 else ((n + H - 6) // 2, -1)

        def has_pair(b, off):
            return not isinstance(b, int) or 0 <= b + off < B

        def part3_pe(pe):
            w = u3
            pe.wait_ge(w3_lo, 2 * len(W3))
            pe.wait_ge(tables_made, 3)

            def use_g(b, has, key):
                use = use_of(USES3, b, has, key)
                if use is None:
                    return
                name, off, _, by_act, by_dve = use
                pe.wait_ge(w.g_hi, by_act)
                pe.wait_ge(w.g_lo, by_dve)
                nb = b + off
                if name[:7] == "experts":
                    half = int(name[7])
                    pe.wait_ge(cs_lo, nb * PAIRS + 2 * half + 2)
                    pe.wait_ge(es_lo, nb * PAIRS + 2 * half + 2)
                    for t in range(NT):
                        tt = slice(t * P, t * P + P)
                        for e in range(E // 2):
                            for k, (l, r) in enumerate(terms(comb_s[:, 0, e, tt], comb_s[:, 1, e, tt],
                                                             eo_s[:, 0, e, :], eo_s[:, 1, e, :])):
                                last = nc.tensor.matmul(halves(ps_g)[:, t, :], l, r, start=e == 0 and k == 0,
                                                        stop=e == E // 2 - 1 and k == 2)
                elif name[0] == "v":
                    t, half = int(name[1]) % 2, int(name[1]) // 2
                    pe.wait_ge(w.ctx_lo_made, nb + 1)
                    tt, m = slice(t * P, t * P + P), slice(half * 512, half * 512 + 512)
                    prods = [p for c in range(2) for p in terms(w.ctxT_hi[:, c, tt], w.ctxT_lo[:, c, tt],
                                                                wv1[:, 0, c, m], wv1[:, 1, c, m])]
                    for k, (l, r) in enumerate(prods):
                        last = nc.tensor.matmul(ps_g, l, r, start=k == 0, stop=k == 5)
                elif name[:4] == "pair":
                    p = int(name[4])
                    pe.wait_ge(w.ctx_lo_made, nb + 1)
                    cols = slice(p * P, p * P + P)
                    for i, (wt, hi, lo) in enumerate(((wq1, w.xT_hi, w.xT_lo), (wk1, w.ctxT_hi, w.ctxT_lo))):
                        prods = [x for c in range(2) for x in terms(wt[:, 0, c, cols], wt[:, 1, c, cols],
                                                                    hi[:, c, :], lo[:, c, :])]
                        for k, (l, r) in enumerate(prods):
                            last = nc.tensor.matmul(halves(ps_g)[:, i, :], l, r, start=k == 0, stop=k == 5)
                elif name == "xT":
                    pe.wait_ge(w.xn_made, nb + 1)
                    last = pe_transposes(w.xn, ps_g)
                elif name == "shift":
                    pe.wait_ge(x3n_made, nb + 1)
                    last = pe_transposes(x3n, ps_g)
                elif name == "mix_k":
                    pe.wait_ge(mix_lo_made, nb + 1)
                    for m in range(DT):
                        mm = slice(m * P, m * P + P)
                        prods = [x for c in range(DT) for x in terms(wf[:, 0, 1, c, mm], wf[:, 1, 1, c, mm],
                                                                     mix_hi[:, 1, c, :], mix_lo[:, 1, c, :])]
                        for k, (l, r) in enumerate(prods):
                            last = nc.tensor.matmul(halves(ps_g)[:, m, :], l, r, start=k == 0, stop=k == 5)
                else:
                    if name == "mix_v":
                        pe.wait_ge(ka_lo_made, nb + 1)
                    i, hi, lo = (0, mix_hi[:, 0], mix_lo[:, 0]) if name == "mix_r" else (2, ka_hi, ka_lo)
                    for t in range(NT):
                        tt = slice(t * P, t * P + P)
                        prods = [x for c in range(DT) for x in terms(hi[:, c, tt], lo[:, c, tt],
                                                                     wf[:, 0, i, c, :], wf[:, 1, i, c, :])]
                        for k, (l, r) in enumerate(prods):
                            last = nc.tensor.matmul(halves(ps_g)[:, t, :], l, r, start=k == 0, stop=k == 5)
                last.then_inc(w.g_ready, 1)

            def scores(b, has, n):
                p, r = n // 2, slice(HD1 * (n % 2), HD1 * (n % 2) + HD1)
                if n % 2 == 0:
                    if p < 2:
                        pe.wait_ge(w.g_lo, base_of(USES3, b)[2] - 1 + p)
                    else:
                        pe.wait_ge(w.g_lo, use_of(USES3, b, has, (2 * p - 4, 1))[4] + 1)
                pe.wait_ge(w.exp_ready, since(unit3(b, n) - 1))
                bank = halves(ps_s[:, n % 2, :])
                for q in range(NT):
                    qq = slice(q * P, q * P + P)
                    for k, (l, rr) in enumerate(terms(qk_hi[r, p % 2, 0, qq], qk_lo[r, p % 2, 0, qq],
                                                      qk_hi[r, p % 2, 1, :], qk_lo[r, p % 2, 1, :])):
                        last = nc.tensor.matmul(bank[:, q, :], l, rr, start=k == 0, stop=k == 2)
                last.then_inc(w.scores_ready, 1)

            def product(b, has, n):
                h, nb = (n, b) if n >= 0 else (n + H, b - 1)
                p = h // 2
                pe.wait_ge(w.prob_lo_ready, unit3(b, n) + 1)
                if h % 2 == 0:
                    pe.wait_ge(w.oT_lo_ready, since(nb * HP + p - 1))
                if h == 0:
                    pe.wait_ge(w.g_lo, base_of(USES3, b)[2])
                if h == H // 2:
                    pe.wait_ge(w.g_lo, use_of(USES3, b, has, (9, 1))[4] + 1)
                cols = slice(p * P, p * P + P)
                prods = [x for k in range(NT) for x in terms(v1_hi[:, k, cols], v1_lo[:, k, cols],
                                                             w.prob_hi[:, n % 2, k, :], w.prob_lo[:, n % 2, k, :])]
                for k, (l, r) in enumerate(prods):
                    last = nc.tensor.matmul(halves(ps_o[:, p % 2, :])[:, h % 2, :], l, r, start=k == 0, stop=k == 5)
                last.then_inc(w.pv_done, 1)

            def turn(b, has):
                for n in range(H):
                    if unit3(b, n) is not None:
                        scores(b, has, n)
                    if unit3(b, n - 2) is not None:
                        pe_unit_transposes(pe, w, unit3(b, n - 2), (n - 2) % 4)
                    if n % 2 == 1:
                        p, off = pair_of(n - 1)
                        if has_pair(b, off):
                            pe_out_proj(pe, w, b + off, p, HP, wo1)
                    use_g(b, has, (n, 0))
                    if unit3(b, n - 4) is not None:
                        product(b, has, n - 4)
                    use_g(b, has, (n, 1))

            turns(pe, turn)

        def part3_act(act):
            w = u3
            def copy_g(b, has, key):
                use = use_of(USES3, b, has, key)
                if use is None or not USES3[key][2]:
                    return
                name, off, number, _, _ = use
                nb = b + off
                act.wait_ge(w.g_ready, number + 1)
                if name[0] == "v":
                    t, half = int(name[1]) % 2, int(name[1]) // 2
                    act.wait_ge(w.pv_done, since(nb * H - (H // 2 if half == 0 else 0)))
                    nc.scalar.activation(v1_hi[:, t, half * 512:half * 512 + 512], ps_g, ACT.Copy).then_inc(w.g_hi, 1)
                elif name[:4] == "pair":
                    p = int(name[4])
                    act.wait_ge(w.scores_ready, since(nb * H + 2 * p - 2))
                    nc.scalar.activation(qk_hi[:, p % 2, :, :], halves(ps_g), ACT.Copy).then_inc(w.g_hi, 1)
                elif name == "xT":
                    nc.scalar.activation(w.xT_hi[:, :, :], halves(ps_g), ACT.Copy).then_inc(w.g_hi, 1)
                elif name == "shift":
                    act.wait_ge(mix_made, nb)
                    nc.scalar.activation(xs[:, :, 1:N + 1], halves(ps_g), ACT.Copy).then_inc(w.g_hi, 1)
                else:
                    act.wait_ge(ka_lo_made, nb)
                    nc.scalar.activation(scratch[:, 0, :, :], halves(ps_g), ACT.Relu).then_inc(w.g_hi, 1)

            def turn(b, has):
                for n in range(H):
                    copy_g(b, has, (n - 1, 1))
                    if unit3(b, n - 3) is not None:
                        act_unit_hi(act, w, unit3(b, n - 3), (n - 3) % 4)
                    if n % 2 == 0:
                        p, off = pair_of(n)
                        if has_pair(b, off):
                            act.wait_ge(w.pv_done, (b + off) * H + 2 * p + 2)
                            act.wait_ge(w.oproj_done, since((b + off) * HP + p - 1))
                            for i in range(2):
                                r = slice(HD1 * i, HD1 * i + HD1)
                                last = nc.scalar.activation(w.oT_hi[r, p % 2, :], halves(ps_o[:, p % 2, :])[r, i, :],
                                                            ACT.Copy)
                            last.then_inc(w.oT_hi_ready, 1)
                    if unit3(b, n) is not None:
                        act_unit_exp(act, w, unit3(b, n), n % 4)
                    copy_g(b, has, (n, 0))
                    if n in SPLIT_STEPS and 1 in has:
                        c = SPLIT_STEPS.index(n)
                        ee, to = slice(2 * c, 2 * c + 2), slice(2 * (c % 2), 2 * (c % 2) + 2)
                        act.wait_ge(comb_loaded, b * 16 + 32)
                        if c < 2:
                            act.wait_ge(w.g_ready, base_of(USES3, b)[0])
                        else:
                            act.wait_ge(w.g_ready, use_of(USES3, b, has, (2, 0))[2] + 1)
                        nc.scalar.activation(comb_s[:, 0, to, :], comb_raw[:, ee, :], ACT.Copy).then_inc(cs_hi, 1)
                        act.wait_ge(eo_loaded, b * 16 + 32)
                        nc.scalar.activation(eo_s[:, 0, to, :], eo_raw[:, ee, :], ACT.Copy).then_inc(cs_hi, 1)
                    if n == 9 and -1 in has:
                        act.wait_ge(mix_made, b)
                        act.wait_ge(w.g_ready, base_of(USES3, b)[0])
                        nc.scalar.activation(mix_hi[:, :, :, :], mixed[:, :, :, :], ACT.Copy).then_inc(mix_hi_made, 1)
                    if n == 11 and 1 in has:
                        act.wait_ge(w.ctx_loaded, b * 16 + 32)
                        if 0 in has:
                            act.wait_ge(w.g_ready, use_of(USES3, b, has, (10, 1))[2] + 1)
                        nc.scalar.activation(w.ctxT_hi[:, :, :], w.ctxT[:, :, :], ACT.Copy).then_inc(w.ctx_hi_made, 1)
                    if n == 14 and -1 in has:
                        act.wait_ge(ksq_done, b)
                        nc.scalar.activation(ka_hi[:, :, :], scratch[:, 1, :, :], ACT.Copy).then_inc(ka_hi_made, 1)
                        act.wait_ge(w.g_lo, use_of(USES3, b, has, (13, 0))[4] + 1)
                        nc.scalar.activation(gate[:, :, :], gate[:, :, :], ACT.Exp).then_inc(gate_exp, 1)
                if -1 in has:
                    act.wait_ge(out_made, b)
                    act.dma_start(out[b - 1, :, :].rearrange("(t p) d -> p t d", p=P), y_out[:, :, :]).then_inc(out_stored, 16)

            turns(act, turn)
            act.wait_ge(out_stored, 16 * B)

        def part3_dve(dve):
            w = u3
            dve.wait_ge(tables_loaded, 32)
            nc.vector.memset(xs[:, :, 0:1], 0.0).then_inc(tables_made, 1)
            for i in range(2):
                nc.vector.tensor_scalar(mu[:, i, 1, :], mu[:, i, 0, :], -1.0, 1.0, ALU.mult, ALU.add).then_inc(tables_made, 1)

            def read_g(b, has, key):
                use = use_of(USES3, b, has, key)
                if use is None or not USES3[key][3]:
                    return
                name, off, number, by_act, _ = use
                nb = b + off
                if USES3[key][2]:
                    dve.wait_ge(w.g_hi, by_act + 1)
                else:
                    dve.wait_ge(w.g_ready, number + 1)
                if name == "experts0":
                    dve.wait_ge(w.x_loaded, nb * 16 + 16)
                    dve.wait_ge(x2_made, nb)
                    nc.vector.tensor_tensor(x2_half[:, :, :], halves(ps_g), w.x_in[:, :, :], ALU.add).then_inc(w.g_lo, 1)
                elif name == "experts1":
                    dve.wait_ge(x2_biased, nb)
                    dve.wait_ge(w.g_lo, use_of(USES3, b, has, (2, 0))[4] + 1)
                    nc.vector.tensor_tensor(x2[:, :, :], halves(ps_g), x2_half[:, :, :], ALU.add).then_inc(w.g_lo, 1)
                elif name[0] == "v":
                    t, half = int(name[1]) % 2, int(name[1]) // 2
                    m = slice(half * 512, half * 512 + 512)
                    dve_lo(v1_lo[:, t, m], ps_g, v1_hi[:, t, m]).then_inc(w.g_lo, 1)
                elif name[:4] == "pair":
                    p = int(name[4])
                    dve_lo(qk_lo[:, p % 2, :, :], halves(ps_g), qk_hi[:, p % 2, :, :]).then_inc(w.g_lo, 1)
                elif name == "xT":
                    dve_lo(w.xT_lo[:, :, :], halves(ps_g), w.xT_hi[:, :, :]).then_inc(w.g_lo, 1)
                elif name == "mix_r":
                    dve.wait_ge(out_made, nb)
                    nc.vector.tensor_scalar(gate[:, :, :], halves(ps_g), -1.0, EXP_MAX, ALU.mult, ALU.min).then_inc(w.g_lo, 1)
                else:
                    dve.wait_ge(gate_step, nb * 2 + 2)
                    nc.vector.tensor_tensor(gate[:, :, :], halves(ps_g), gate[:, :, :], ALU.mult).then_inc(w.g_lo, 1)

            def turn(b, has):
                for n in range(H):
                    if unit3(b, n) is not None:
                        dve_unit_max(dve, w, unit3(b, n), n % 4)
                    if unit3(b, n - 1) is not None:
                        dve_unit_inv(dve, w, unit3(b, n - 1), (n - 1) % 4)
                    read_g(b, has, (n - 1, 1))
                    if unit3(b, n - 3) is not None:
                        dve_unit_lo(dve, w, unit3(b, n - 3), (n - 3) % 4)
                    if n % 2 == 0:
                        p, off = pair_of(n)
                        if has_pair(b, off):
                            dve.wait_ge(w.oT_hi_ready, (b + off) * HP + p + 1)
                            for i in range(2):
                                r = slice(HD1 * i, HD1 * i + HD1)
                                last = dve_lo(w.oT_lo[r, p % 2, :], halves(ps_o[:, p % 2, :])[r, i, :],
                                              w.oT_hi[r, p % 2, :])
                            last.then_inc(w.oT_lo_ready, 1)
                    read_g(b, has, (n, 0))
                    if n in SPLIT_STEPS and 1 in has:
                        c = SPLIT_STEPS.index(n)
                        ee, to = slice(2 * c, 2 * c + 2), slice(2 * (c % 2), 2 * (c % 2) + 2)
                        dve.wait_ge(cs_hi, (b + 1) * 2 * PAIRS + 2 * c + 1)
                        dve_lo(comb_s[:, 1, to, :], comb_raw[:, ee, :], comb_s[:, 0, to, :]).then_inc(cs_lo, 1)
                    if n == 5 and -1 in has:
                        dve.wait_ge(w.oproj_done, b * HP)
                        dve.wait_ge(out_made, b - 1)
                        nc.vector.tensor_tensor(x3[:, :, :], halves(ps_y), x2_res[:, :, :], ALU.add).then_inc(w.sum_taken, 1)
                        dve.wait_ge(w.sum_taken, b)
                        for k in range(2):
                            dve_ln(dve, x3_norm, x3, (b - 1) * LN_STEPS, k)
                    if n == 5 and 0 in has:
                        dve.wait_ge(x2_biased, b + 1)
                        nc.vector.tensor_copy(x2_res[:, :, :], x2_bias[:, :, :]).then_inc(x2_moved, 1)
                    if n == 6 and -1 in has:
                        for k in range(2, 5):
                            dve_ln(dve, x3_norm, x3, (b - 1) * LN_STEPS, k)
                        dve.wait_ge(w.g_ready, base_of(USES3, b)[0])
                        dve_normed(x3_norm, x3, x3n).then_inc(x3n_made, 1)
                    if n == 6 and 1 in has:
                        dve.wait_ge(w.g_lo, use_of(USES3, b, has, (5, 1))[4] + 1)
                        dve.sem_inc(x2_made, 1)
                    if n in (7, 8) and 1 in has:
                        for k in range(2):
                            dve_ln(dve, x2_norm, x2, (b + 1) * LN_STEPS, 2 * (n - 7) + k)
                    if n == 10 and 1 in has:
                        dve_ln(dve, x2_norm, x2, (b + 1) * LN_STEPS, 4)
                        dve.wait_ge(w.g_ready, base_of(USES3, b)[0])
                        dve_normed(x2_norm, x2, w.xn).then_inc(w.xn_made, 1)
                    if n == 8 and -1 in has:
                        dve.wait_ge(w.g_hi, use_of(USES3, b, has, (7, 1))[3] + 1)
                        dve.wait_ge(ka_lo_made, b - 1)
                        for i in (1, 0):
                            for c in range(DT):
                                last = nc.vector.tensor_scalar(scratch[:, i, c, :], xs[:, c, 0:N], mu[:, i, 1, c:c + 1],
                                                               None, ALU.mult)
                        last.then_inc(mix_part_made, 1)
                    if n == 9 and -1 in has:
                        dve.wait_ge(mix_part_made, b)
                        dve.wait_ge(mix_lo_made, b - 1)
                        for i in (1, 0):
                            for c in range(DT):
                                last = nc.vector.scalar_tensor_tensor(mixed[:, i, c, :], xs[:, c, 1:N + 1],
                                                                      mu[:, i, 0, c:c + 1], scratch[:, i, c, :],
                                                                      ALU.mult, ALU.add)
                        last.then_inc(mix_made, 1)
                    if n == 13 and -1 in has:
                        dve.wait_ge(w.g_hi, use_of(USES3, b, has, (12, 0))[3] + 1)
                        nc.vector.tensor_tensor(scratch[:, 1, :, :], scratch[:, 0, :, :], scratch[:, 0, :, :],
                                                ALU.mult).then_inc(ksq_done, 1)
                    if n == 14 and -1 in has:
                        dve.wait_ge(gate_exp, b)
                        nc.vector.tensor_scalar(gate[:, :, :], gate[:, :, :], 1.0, None, ALU.add).then_inc(gate_step, 1)
                        dve.wait_ge(gate_step, b * 2 - 1)
                        nc.vector.reciprocal(gate[:, :, :], gate[:, :, :]).then_inc(gate_step, 1)
                    if n == 15 and -1 in has:
                        dve.wait_ge(w.g_lo, use_of(USES3, b, has, (15, 0))[4] + 1)
                        dve.wait_ge(out_stored, b * 16 - 16)
                        nc.vector.tensor_tensor(y_out[:, :, :], gate[:, :, :], x3[:, :, :], ALU.add).then_inc(out_made, 1)

            turns(dve, turn)

        def part3_pool(pool):
            w = u3
            pool.wait_ge(tables_loaded, 32)

            def turn(b, has):
                for n in range(H):
                    if unit3(b, n - 1) is not None:
                        pool_unit_norm(pool, w, unit3(b, n - 1), (n - 1) % 4)
                    if n in SPLIT_STEPS and 1 in has:
                        c = SPLIT_STEPS.index(n)
                        ee, to = slice(2 * c, 2 * c + 2), slice(2 * (c % 2), 2 * (c % 2) + 2)
                        pool.wait_ge(cs_hi, (b + 1) * 2 * PAIRS + 2 * c + 2)
                        nc.gpsimd.tensor_tensor(eo_s[:, 1, to, :], eo_raw[:, ee, :], eo_s[:, 0, to, :].bitcast(F32),
                                                ALU.subtract).then_inc(es_lo, 1)
                    if n == 1 and 0 in has:
                        pool.wait_ge(x2_made, b + 1)
                        pool.wait_ge(x2_moved, b)
                        nc.gpsimd.tensor_tensor(x2_bias[:, :, :], x2[:, :, :],
                                                b_out[:, :].unsqueeze(1).to_broadcast([P, NT, D]),
                                                ALU.add).then_inc(x2_biased, 1)
                    if n == 9 and -1 in has:
                        pool.wait_ge(mix_hi_made, b)
                        nc.gpsimd.tensor_tensor(mix_lo[:, :, :, :].rearrange("p i c n -> p (i c n)"),
                                                mixed[:, :, :, :].rearrange("p i c n -> p (i c n)"),
                                                mix_hi[:, :, :, :].rearrange("p i c n -> p (i c n)").bitcast(F32),
                                                ALU.subtract).then_inc(mix_lo_made, 1)
                    if n == 11 and 1 in has:
                        pool.wait_ge(w.ctx_hi_made, b + 2)
                        nc.gpsimd.tensor_tensor(w.ctxT_lo[:, :, :], w.ctxT[:, :, :], w.ctxT_hi[:, :, :].bitcast(F32),
                                                ALU.subtract).then_inc(w.ctx_lo_made, 1)
                    if n == 14 and -1 in has:
                        pool.wait_ge(ka_hi_made, b)
                        nc.gpsimd.tensor_tensor(ka_lo[:, :, :], scratch[:, 1, :, :], ka_hi[:, :, :].bitcast(F32),
                                                ALU.subtract).then_inc(ka_lo_made, 1)

            turns(pool, turn)

        def part3_sp(sp):
            w = u3
            sp.dma_start(mu[:, :, 0, :], a["mu"]).then_inc(tables_loaded, 16)
            sp.dma_start(b_out[:, :], a["b_out"].partition_broadcast(P)).then_inc(tables_loaded, 16)

            def turn(b, has):
                if 1 in has:
                    sp.wait_ge(x2_made, b + 1)
                    sp.sem_inc(sp_passed, 1)
                    sp.dma_start(w.x_in[:, :, :], x1_dram[b + 1, :, :, :]).then_inc(w.x_loaded, 16)
                    sp.wait_ge(cs_lo, (b + 1) * PAIRS)
                    sp.sem_inc(sp_passed, 1)
                    sp.dma_start(comb_raw[:, :, :], comb_dram[b + 1, :, :, :]).then_inc(comb_loaded, 16)
                    sp.wait_ge(es_lo, (b + 1) * PAIRS)
                    sp.sem_inc(sp_passed, 1)
                    sp.dma_start(eo_raw[:, :, :], eo_dram[:, :, b + 1, :].rearrange("e p d -> p e d")).then_inc(eo_loaded, 16)
                    sp.wait_ge(w.ctx_lo_made, b + 1)
                    sp.sem_inc(sp_passed, 1)
                    sp.dma_start(w.ctxT[:, :, :],
                                 a["ctxT"][b + 1, :, :].rearrange("(c p) n -> p c n", c=2)).then_inc(w.ctx_loaded, 16)

            turns(sp, turn)

        @block.tensor
        def _(pe):
            part1_pe(pe)
            end_part(pe, 0)
            part2_pe(pe)
            end_part(pe, 1)
            part3_pe(pe)

        @block.scalar
        def _(act):
            part1_act(act)
            end_part(act, 0)
            part2_act(act)
            end_part(act, 1)
            part3_act(act)

        @block.vector
        def _(dve):
            part1_dve(dve)
            end_part(dve, 0)
            part2_dve(dve)
            end_part(dve, 1)
            part3_dve(dve)

        @block.gpsimd
        def _(pool):
            part1_pool(pool)
            end_part(pool, 0)
            part2_pool(pool)
            end_part(pool, 1)
            part3_pool(pool)

        @block.sync
        def _(sp):
            part1_sp(sp)
            end_part(sp, 0)
            part2_sp(sp)
            end_part(sp, 1)
            part3_sp(sp)


def kernel(**inputs):
    import numpy as np
    import concourse.bacc as bacc
    from concourse.bass_utils import run_bass_kernel_spmd

    i = {k: np.asarray(v) for k, v in inputs.items()}
    heads, dim = 16, i["x"].shape[2]
    hd = dim // heads

    def twice(w):
        w = w.reshape(w.shape[0], heads, 1, hd)
        return np.concatenate([w, w], axis=2).reshape(w.shape[0], 2 * dim)

    wo = i["L0_xattn_Wo"].reshape(4, 4, 1, hd, dim)
    wo = np.concatenate([wo, wo], axis=2).reshape(4, P, dim).transpose(1, 0, 2)
    mu = np.stack([i["L1_ffn_mu_r"], i["L1_ffn_mu_k"]]).reshape(2, 2, P).transpose(2, 0, 1)
    b1 = i["L0_ffn_b1"]
    arrays = {
        "x": i["x"],
        "ctxT": i["ctx_768"].transpose(0, 2, 1),
        "mask": i["mask_BxS2_bf1"].view(np.uint8),
        "Wq0": twice(i["L0_xattn_Wq"]),
        "Wk0": twice(i["L0_xattn_Wk"]),
        "Wv0": i["L0_xattn_Wv"],
        "Wo0": wo,
        "gamma": i["L0_ffn_norm_gamma"],
        "gamma_s": i["L0_ffn_slot_norm_gamma"],
        "lo_rows": np.where(np.arange(P) % 32 >= 16, -1.0, 0.0).astype(np.float32).reshape(P, 1),
        "slots": i["L0_ffn_slot_embeds"],
        "w1": i["L0_ffn_w1"],
        "b1": b1.reshape(b1.shape[0], b1.shape[1] // P, P).transpose(0, 2, 1),
        "w2": i["L0_ffn_w2"],
        "b2": i["L0_ffn_b2"],
        "w_q": i["L1_xattn_w_q"],
        "w_k": i["L1_xattn_w_k"],
        "w_v": i["L1_xattn_w_v"],
        "w_out": i["L1_xattn_w_out"],
        "b_out": i["L1_xattn_b_out"],
        "wf": np.stack([i["L1_ffn_W_r"].T, i["L1_ffn_W_k"].T, i["L1_ffn_W_v"].T]),
        "mu": mu,
    }
    nc = bacc.Bacc("TRN2", target_bir_lowering=False, num_devices=1)
    fed, aps = {}, {}
    for name, v in arrays.items():
        v = np.ascontiguousarray(v)
        fed[f"in_{name}"] = v
        aps[name] = nc.dram_tensor(f"in_{name}", v.shape, mybir.dt.from_np(v.dtype), kind="ExternalInput").ap()
    out = nc.dram_tensor("out", i["x"].shape, F32, kind="ExternalOutput").ap()
    xattn_ffn_kernel(nc, aps, out)
    r = run_bass_kernel_spmd(nc, [fed], core_ids=[0])
    return r.results[0]["out"]
```
